# Optimizing a Trainium2 kernel written in Bass

```python
import numpy as np
import jax
import jax.numpy as jnp

def _softmax(x, axis=-1):
    return jax.nn.softmax(x, axis=axis)

def _gelu(x):
    return jax.nn.gelu(x, approximate=True)

def _silu(x):
    return jax.nn.silu(x)

def _sigmoid(x):
    return jax.nn.sigmoid(x)

def _layernorm(x, axis=-1, eps=1e-05):
    m = jnp.mean(x, axis=axis, keepdims=True)
    v = jnp.var(x, axis=axis, keepdims=True)
    return (x - m) / jnp.sqrt(v + eps)

def _scatter_add(tgt, idx, src, axis=0):
    return tgt.at[idx].add(src)

def _segment_sum(src, seg, n):
    return jax.ops.segment_sum(src, seg, n)
kernel_name = 'mk_decoder_postln_d1_seqx_r4_242853'

def setup_inputs(seed: int=0):
    np.random.seed(seed)
    _w = jnp.asarray

    def _rec_inputs():
        import jax
        import jax.numpy as jnp
        _rk = jax.random.key(seed)
        x = 0.0002417 + 0.9998 * jax.random.normal(jax.random.fold_in(_rk, 1), (8, 112, 256), jnp.float32)
        _lenS = 112 - jax.random.randint(jax.random.fold_in(_rk, 7), (8,), 0, max(1, 112 // 4) + 1, jnp.int32)
        _lenS2 = 375 - jax.random.randint(jax.random.fold_in(_rk, 8), (8,), 0, max(1, 375 // 4) + 1, jnp.int32)
        _ctx_1024P = jax.random.normal(jax.random.fold_in(_rk, 11), (8, 16, 256), jnp.float32)
        _ctx_1024c = jax.random.dirichlet(jax.random.fold_in(_rk, 511), 0.3 * jnp.ones((16,), jnp.float32), (8, 375))
        _ctx_1024t = jnp.einsum('bsk,bkd->bsd', _ctx_1024c, _ctx_1024P)
        _ctx_1024t = _ctx_1024t * jax.lax.rsqrt(jnp.mean(jnp.square(_ctx_1024t)) + 1e-12) * 0.953939
        ctx_1024 = 7.22013e-05 + 1.00017 * (_ctx_1024t + 0.3 * jax.random.normal(jax.random.fold_in(_rk, 611), (8, 375, 256), jnp.float32))
        return (x, ctx_1024)
    x, ctx_1024 = _rec_inputs()

    def _L0_attn_setup():
        import jax, jax.numpy as jnp
        import numpy as np
        B, S, D = (4, 512, 256)
        SCALE = 1.0 / np.sqrt(D)
        key = jax.random.key(seed)
        k1, k2, k3 = jax.random.split(key, 3)
        x = jax.random.normal(k1, (B, S, D), dtype=jnp.float32)
        bound = 1.0 / np.sqrt(D)
        W_qk = jax.random.uniform(k2, (D, D), minval=-bound, maxval=bound, dtype=jnp.float32)
        W_v = jax.random.uniform(k3, (D, D), minval=-bound, maxval=bound, dtype=jnp.float32)
        alibi_slope = jnp.full((1,), 0.5, dtype=jnp.float32)
        return {'x': x, 'W_qk': W_qk, 'W_v': W_v, 'alibi_slope': alibi_slope}
    _L0_attn_all = _L0_attn_setup()
    _L0_attn_in = {k: v for k, v in _L0_attn_all.items() if k in ('W_qk', 'W_v', 'alibi_slope')}
    del _L0_attn_all

    def _L0_xattn_setup():
        import jax, jax.numpy as jnp
        import numpy as np
        D_MODEL = 256
        B, S = (4, 512)
        key = jax.random.key(seed)
        ks = jax.random.split(key, 10)
        s = 1.0 / np.sqrt(D_MODEL)
        return {'k': jax.random.normal(ks[0], (B, S, D_MODEL), jnp.float32), 'v': jax.random.normal(ks[1], (B, S, D_MODEL), jnp.float32), 'q': jax.random.normal(ks[2], (B, S, D_MODEL), jnp.float32), 'Wk': jax.random.normal(ks[3], (D_MODEL, D_MODEL), jnp.float32) * s, 'Wv': jax.random.normal(ks[4], (D_MODEL, D_MODEL), jnp.float32) * s, 'bv': jnp.zeros((D_MODEL,), jnp.float32), 'Wq': jax.random.normal(ks[5], (D_MODEL, D_MODEL), jnp.float32) * s, 'bq': jnp.zeros((D_MODEL,), jnp.float32), 'Wo': jax.random.normal(ks[6], (D_MODEL, D_MODEL), jnp.float32) * s, 'bo': jnp.zeros((D_MODEL,), jnp.float32)}
    _L0_xattn_all = _L0_xattn_setup()
    _L0_xattn_in = {k: v for k, v in _L0_xattn_all.items() if k in ('Wk', 'Wv', 'bv', 'Wq', 'bq', 'Wo', 'bo')}
    del _L0_xattn_all

    def _L0_ffn_setup():
        import jax, jax.numpy as jnp
        import numpy as np
        D_MODEL = 256
        D_FF = 1024
        NUM_EXPERTS = 8
        key = jax.random.key(seed)
        ks = jax.random.split(key, 8)
        scale_in = 1.0 / np.sqrt(D_MODEL)
        scale_ff = 1.0 / np.sqrt(D_FF)
        x = jax.random.normal(ks[0], (4, 512, D_MODEL), dtype=jnp.float32)
        gate_w = jax.random.uniform(ks[1], (NUM_EXPERTS, D_MODEL), jnp.float32, -scale_in, scale_in)
        gate_b = jax.random.uniform(ks[2], (NUM_EXPERTS,), jnp.float32, -scale_in, scale_in)
        expert_bias = jnp.zeros((NUM_EXPERTS,), dtype=jnp.float32)
        w1 = jax.random.uniform(ks[3], (NUM_EXPERTS, D_MODEL, D_FF), jnp.float32, -scale_in, scale_in)
        b1 = jax.random.uniform(ks[4], (NUM_EXPERTS, D_FF), jnp.float32, -scale_in, scale_in)
        w2 = jax.random.uniform(ks[5], (NUM_EXPERTS, D_FF, D_MODEL), jnp.float32, -scale_ff, scale_ff)
        b2 = jax.random.uniform(ks[6], (NUM_EXPERTS, D_MODEL), jnp.float32, -scale_ff, scale_ff)
        return {'x': x, 'gate_w': gate_w, 'gate_b': gate_b, 'expert_bias': expert_bias, 'w1': w1, 'b1': b1, 'w2': w2, 'b2': b2}
    _L0_ffn_all = _L0_ffn_setup()
    _L0_ffn_in = {k: v for k, v in _L0_ffn_all.items() if k in ('gate_w', 'gate_b', 'expert_bias', 'w1', 'b1', 'w2', 'b2')}
    del _L0_ffn_all
    return {'x': x, 'ctx_1024': ctx_1024, 'L0_attn_W_qk': _L0_attn_in['W_qk'], 'L0_attn_W_v': _L0_attn_in['W_v'], 'L0_attn_alibi_slope': _L0_attn_in['alibi_slope'], 'L0_xattn_Wk': _L0_xattn_in['Wk'], 'L0_xattn_Wv': _L0_xattn_in['Wv'], 'L0_xattn_bv': _L0_xattn_in['bv'], 'L0_xattn_Wq': _L0_xattn_in['Wq'], 'L0_xattn_bq': _L0_xattn_in['bq'], 'L0_xattn_Wo': _L0_xattn_in['Wo'], 'L0_xattn_bo': _L0_xattn_in['bo'], 'L0_ffn_gate_w': _L0_ffn_in['gate_w'], 'L0_ffn_gate_b': _L0_ffn_in['gate_b'], 'L0_ffn_expert_bias': _L0_ffn_in['expert_bias'], 'L0_ffn_w1': _L0_ffn_in['w1'], 'L0_ffn_b1': _L0_ffn_in['b1'], 'L0_ffn_w2': _L0_ffn_in['w2'], 'L0_ffn_b2': _L0_ffn_in['b2']}

def reference(x, ctx_1024, L0_attn_W_qk, L0_attn_W_v, L0_attn_alibi_slope, L0_xattn_Wk, L0_xattn_Wv, L0_xattn_bv, L0_xattn_Wq, L0_xattn_bq, L0_xattn_Wo, L0_xattn_bo, L0_ffn_gate_w, L0_ffn_gate_b, L0_ffn_expert_bias, L0_ffn_w1, L0_ffn_b1, L0_ffn_w2, L0_ffn_b2):
    import jax
    import jax.numpy as jnp

    def _L0_attn_ref(x, W_qk, W_v, alibi_slope):
        import jax, jax.numpy as jnp
        import numpy as np
        B, S, D = (4, 512, 256)
        SCALE = 1.0 / np.sqrt(D)
        seq_len = x.shape[1]
        scores = jnp.einsum('bqe,bke->bqk', x @ W_qk, x) * SCALE
        kpos = jnp.arange(seq_len, dtype=x.dtype)[None, :]
        qpos = jnp.arange(seq_len, dtype=x.dtype)[:, None]
        scores = scores + (kpos - qpos) * alibi_slope[0]
        causal = qpos >= kpos
        scores = jnp.where(causal, scores, -jnp.inf)
        attn = jax.nn.softmax(scores, axis=-1)
        v = x @ W_v.T
        return jnp.einsum('bqk,bkd->bqd', attn, v)

    def _L0_xattn_ref(k, v, q, Wk, Wv, bv, Wq, bq, Wo, bo):
        import jax, jax.numpy as jnp
        import numpy as np
        D_MODEL = 256
        B, S = (4, 512)
        kp = jnp.einsum('bsd,ed->bse', k, Wk)
        vp = jnp.einsum('bsd,ed->bse', v, Wv) + bv
        qp = jnp.einsum('bsd,ed->bse', q, Wq) + bq
        scale = 1.0 / jnp.sqrt(jnp.float32(kp.shape[-1]))
        scores = jnp.einsum('bqd,bkd->bqk', qp, kp) * scale
        probs = jax.nn.softmax(scores, axis=-1)
        ctx = jnp.einsum('bqk,bkd->bqd', probs, vp)
        return jnp.einsum('bqd,ed->bqe', ctx, Wo) + bo

    def _L0_ffn_ref(x, gate_w, gate_b, expert_bias, w1, b1, w2, b2):
        import jax, jax.numpy as jnp
        import numpy as np
        D_MODEL = 256
        D_FF = 1024
        NUM_EXPERTS = 8
        gate_logits = jnp.einsum('bsd,ed->bse', x, gate_w) + gate_b + expert_bias
        top_idx = jnp.argmax(gate_logits, axis=-1)
        out = jnp.zeros_like(x)
        for e in range(NUM_EXPERTS):
            mask = (top_idx == e)[..., None].astype(x.dtype)
            h = jax.nn.relu(jnp.einsum('bsd,df->bsf', x, w1[e]) + b1[e])
            y = jnp.einsum('bsf,fd->bsd', h, w2[e]) + b2[e]
            out = out + mask * y
        return out
    x = _layernorm(x + _L0_attn_ref(x, L0_attn_W_qk, L0_attn_W_v, L0_attn_alibi_slope), axis=-1)
    x = _layernorm(x + _L0_xattn_ref(ctx_1024, ctx_1024, x, L0_xattn_Wk, L0_xattn_Wv, L0_xattn_bv, L0_xattn_Wq, L0_xattn_bq, L0_xattn_Wo, L0_xattn_bo), axis=-1)
    x = _layernorm(x + _L0_ffn_ref(x, L0_ffn_gate_w, L0_ffn_gate_b, L0_ffn_expert_bias, L0_ffn_w1, L0_ffn_b1, L0_ffn_w2, L0_ffn_b2), axis=-1)
    return x

_drawn_inputs = setup_inputs


def setup_inputs(seed=0):
    import zlib

    import numpy as np

    out = dict(_drawn_inputs(seed))
    spreads = {'L0_xattn_bv': (0.0, 0.1),
     'L0_xattn_bq': (0.0, 0.1),
     'L0_xattn_bo': (0.0, 0.1),
     'L0_ffn_expert_bias': (0.0, 0.1)}
    factors = {'L0_ffn_b1': 3.987, 'L0_ffn_b2': 3.167}
    for name, (base, spread) in spreads.items():
        noise = np.random.default_rng([zlib.crc32(name.encode()), seed]).standard_normal(out[name].shape)
        drawn = base * np.exp(spread * noise) if base else spread * noise
        out[name] = jnp.asarray(drawn.astype(out[name].dtype))
    for name, factor in factors.items():
        out[name] = (out[name] * factor).astype(out[name].dtype)
    return out
```

```python
from contextlib import ExitStack

import concourse.bass as bass
from concourse import mybir

F32 = mybir.dt.float32
BF16 = mybir.dt.bfloat16
F16 = mybir.dt.float16
I32 = mybir.dt.int32
U32 = mybir.dt.uint32
ALU = mybir.AluOpType
ACT = mybir.ActivationFunctionType
AX = mybir.AxisListType

P = 128
MASKED = -1.0e30
EPS = 1e-5
DROP = 4096


def decoder_layer(nc, x, ctx_in, w_qk, w_v, slope, wk, w_xv, bv, wq, bq, wo, bo,
                  gate_w, gate_b, expert_bias, w1, b1, w2, b2, out):
    B, S, D = x.shape
    SK = ctx_in.shape[1]
    E, _, F = w1.shape
    DC = D // P
    KC = 3
    SP_ = SK // KC
    FC = F // P
    FH = F // 2
    N = B * S
    TILES = -(-N // P)
    SLOTS = TILES + E - 1
    COLS = SLOTS + 2
    WE = 2 * DC * F
    BR = F + D
    SCALE = float(D) ** -0.5
    assert S <= P and SP_ * KC == SK and SP_ <= P and DC == 2 and FC * D == DC * F

    with ExitStack() as stack:
        def sb(name, shape, dt=F32):
            return stack.enter_context(nc.sbuf_tensor(name, shape, dt))

        def sem(name):
            return stack.enter_context(nc.semaphore(name))

        x2_rows = nc.dram_tensor("x2_rows", [N, D], F32, kind="Internal").ap()
        bias_parts = nc.dram_tensor("bias_parts", [3, E, BR], BF16, kind="Internal").ap()

        w_ex = sb("w_ex", [P, E * WE])
        bias_rows = sb("bias_rows", [P, E * BR], BF16)
        ident = sb("ident", [P, P])
        ones = sb("ones", [P, P])
        ones3 = sb("ones3", [P, P], BF16)
        alibi = sb("alibi", [S, S])
        iota_i = sb("iota_i", [P, 3 * P], I32)
        wqk_s = sb("wqk_s", [P, DC, D])
        wvT = sb("wvT", [P, DC, D])
        a_x = sb("a_x", [P, DC, D])
        m_x = sb("m_x", [P, DC, D])
        c_x = sb("c_x", [P, DC])
        b_x = sb("b_x", [S, D])
        gwT = sb("gwT", [P, DC, E])
        gb = sb("gb", [S, E])
        shared = sb("shared", [P, 4480])
        raw = shared[:, 0:5 * DC * D].rearrange("p (n c d) -> p n c d", n=5, c=DC)
        raw_wv, raw_wo, raw_wq, raw_wk, raw_xv = (raw[:, n] for n in range(5))
        woT = shared[:, 2560:3072].rearrange("p (c d) -> p c d", c=DC)
        bst = shared[0:E, 3072:3072 + BR]
        gw_raw = sb("gw_raw", [E, D])
        gb_raw = sb("gb_raw", [S, 2, E])
        bq_col = sb("bq_col", [P, DC])
        bv_col = sb("bv_col", [P, DC])
        bv_wide = sb("bv_wide", [P, DC, S])
        bo_row = sb("bo_row", [1, D])
        slope_c = sb("slope_c", [S, 1])
        xs = sb("xs", [S, D])
        xw = sb("xw", [S, D])
        cs = sb("cs", [SP_, KC * D])
        sc = sb("sc", [S, S])
        pr = sb("pr", [S, S])
        pT = sb("pT", [S, S])
        y1 = sb("y1", [S, D])
        x1 = sb("x1", [S, D])
        x1b = sb("x1b", [S, D])
        x2 = sb("x2", [S, D])
        x2T = sb("x2T", [P, DC, S])
        late = [(E - 1) * WE]

        def borrow(rows, *shape):
            n = shape[0] * (shape[1] if len(shape) == 2 else 1)
            v = w_ex[0:rows, late[0]:late[0] + n]
            late[0] += n
            assert late[0] <= E * WE
            return v.rearrange("p (a b) -> p a b", b=shape[1]) if len(shape) == 2 else v

        cw = borrow(SP_, KC, D)
        xT = borrow(P, DC, S)
        gT = borrow(P, DC, S)
        uT = borrow(P, DC, S)
        x1T = borrow(P, DC, S)
        rT = borrow(P, DC, S)
        cT = borrow(P, DC, SK)
        pc = borrow(S, SK)
        pcT = borrow(SP_, KC, S)
        ccT = borrow(P, DC, S)
        y2 = borrow(S, D)
        st = sb("st", [P, 64])
        logit = sb("logit", [S, B, E])
        rt = sb("rt", [S, 2200])
        bpart = rt[0:E, 0:3 * BR // 2].bitcast(BF16).rearrange("p (n f) -> p n f", n=3)
        oh16 = sb("oh16", [S, B, E], BF16)
        ohs16 = sb("ohs16", [S, E], BF16)
        low16 = sb("low16", [S, P], BF16)
        ones16 = sb("ones16", [S, P], BF16)
        place16 = sb("place16", [S, B, P], F16)
        slot16 = sb("slot16", [S, B, 2, COLS], F16)
        row_in = sb("row_in", [P, COLS], I32)
        row_out = sb("row_out", [P, COLS], I32)
        slot_expert = sb("slot_expert", [1, COLS], I32)
        slots_used = sb("slots_used", [1, 2], I32)
        idx_in = [sb(f"idx_in{u}", [P, 1], I32) for u in range(2)]
        idx_out = [sb(f"idx_out{u}", [P, 1], I32) for u in range(2)]

        hid = shared[:, 0:F]
        hidT = shared[:, F:2 * F].rearrange("p (c n) -> p c n", c=FC)
        xg = [shared[:, 2048 + D * u:2048 + D * u + D] for u in range(2)]
        xgT = shared[:, 2560:2816].rearrange("p (c n) -> p c n", c=DC)
        y3 = shared[:, 2816:3072]
        y3n = [shared[:, 3072 + D * u:3072 + D * u + D] for u in range(2)]

        bank = [stack.enter_context(nc.psum_tensor(f"bank{n}", [P, 512], F32)) for n in range(8)]

        def cols2(b, n=S):
            return bank[b][:, 0:DC * n].rearrange("p (c n) -> p c n", c=DC)

        names = """weights_in small_in xs_in cs_in experts_in x_copied c_copied ident_ready ones_ready
            alibi_flat alibi_ready wide_ready tables_ready
            wvT_psum wvT_ready woT_psum woT_ready gwT_psum gwT_ready a_psum a_ready m_psum m_ready c_psum
            c_ready bx_psum bx_ready bias_split bias_stored bias_in bias_zeroed
            xT_psum xT_ready gT_psum gT_ready sc_psum sc_biased sc_max p_ready p_inv pT_psum pT_ready
            uT_psum uT_ready out1_psum y1_ready y1_bn y1_agg y1_stats y1_rstd x1_ready x1b_ready
            x1T_psum x1T_ready rT_psum rT_ready cT_psum cT_ready sc2_psum sc2_max pc_ready pc_inv
            pcT_psum pcT_ready ccT_psum ccT_ready out2_psum y2_ready y2_bn y2_agg y2_stats y2_rstd x2_ready x2_stored
            x2T_psum x2T_ready gate_psum logit_ready
            route hot_ready rank_psum table16_ready table_psum used_ready
            idx_ready0 idx_ready1 oidx_ready0 oidx_ready1 gathered0 gathered1 xgT_psum xgT_ready h0_psum h1_psum h0_ready h1_ready
            hT0_psum hT1_psum hT0_ready hT1_ready y3_psum y3_ready y3_bn y3_agg y3_stats y3_rstd o_ready
            scattered0 scattered1 passed""".split()
        s = {n: sem(n) for n in names}
        gathered = [s["gathered0"], s["gathered1"]]
        scattered = [s["scattered0"], s["scattered1"]]
        idx_ready = [s["idx_ready0"], s["idx_ready1"]]
        oidx_ready = [s["oidx_ready0"], s["oidx_ready1"]]

        def wait(e, name, n):
            if not (isinstance(n, int) and n <= 0):
                e.wait_ge(s[name], n)

        def waited(e):
            e.sem_inc(s["passed"], 1)

        block = stack.enter_context(nc.Block())

        @block.sync
        def _(sp):
            def load_x(i):
                wait(sp, "x_copied", i)
                sp.dma_start(xs[:, :], x[bass.ds(i, 1), :, :].rearrange("o s d -> (o s) d")).then_inc(s["xs_in"], 16)

            def load_ctx(c):
                wait(sp, "c_copied", c)
                sp.dma_start(cs[:, :], ctx_in[bass.ds(c, 1), :, :].rearrange("o (p c) d -> (o p) (c d)", c=KC)).then_inc(s["cs_in"], 16)

            def store_x2(c):
                wait(sp, "x2_ready", c + 1)
                sp.dma_start(x2_rows[bass.ds(c * S, S), :], x2[:, :]).then_inc(s["x2_stored"], 16)

            load_x(0)
            sp.dma_start(wqk_s[:, :, :], w_qk.rearrange("(c p) e -> p c e", p=P)).then_inc(s["weights_in"], 16)
            for dst, src in ((raw_wv, w_v), (raw_wo, wo), (raw_wq, wq), (raw_wk, wk), (raw_xv, w_xv)):
                sp.dma_start(dst, src.rearrange("(c p) e -> p c e", p=P)).then_inc(s["weights_in"], 16)
            load_ctx(0)
            load_x(1)
            load_ctx(1)
            with sp.Fori(2, B) as i:
                load_x(i)
                store_x2(i - 2)
                load_ctx(i)
            store_x2(B - 2)
            store_x2(B - 1)

        @block.gpsimd
        def _(pool):
            for dst, src in ((gw_raw[:, :], gate_w), (bst[:, 0:F], b1), (bst[:, F:BR], b2),
                             (gb_raw[:, 0, :], gate_b.partition_broadcast(S)),
                             (gb_raw[:, 1, :], expert_bias.partition_broadcast(S)),
                             (slope_c[:, :], slope.partition_broadcast(S)),
                             (bo_row[:, :], bo.rearrange("(o d) -> o d", o=1)),
                             (bq_col[:, :], bq.rearrange("(c p) -> p c", p=P)),
                             (bv_col[:, :], bv.rearrange("(c p) -> p c", p=P))):
                pool.dma_start(dst, src, allow_slow_non_contiguous=True).then_inc(s["small_in"], 16)
            pool.memset(ident[:, :], 0.0).then_inc(s["ident_ready"], 1)
            pool.wait_ge(s["ident_ready"], 1)
            pool.affine_select(out=ident[:, :], in_=ident[:, :], compare_op=ALU.not_equal, fill=1.0, base=0,
                               pattern=[[-1, P]], channel_multiplier=1).then_inc(s["ident_ready"], 1)

            def copy_x(i):
                pool.wait_ge(s["xs_in"], 16 * (i + 1))
                wait(pool, "uT_psum", i)
                wait(pool, "y1_ready", i)
                waited(pool)
                pool.tensor_scalar(xw[:, :], xs[:, :], 1.0, 0.0, ALU.mult, ALU.add).then_inc(s["x_copied"], 1)

            def copy_ctx(c):
                pool.wait_ge(s["cs_in"], 16 * (c + 1))
                wait(pool, "ccT_psum", c)
                waited(pool)
                pool.tensor_scalar(cw.rearrange("p c d -> p (c d)"), cs[:, :], 1.0, 0.0, ALU.mult, ALU.add).then_inc(s["c_copied"], 1)

            def rstd(n, k, rows):
                pool.wait_ge(s[f"y{n}_stats"], k + 1)
                pool.tensor_tensor(st[0:rows, 8 * n + 2:8 * n + 3], st[0:rows, 8 * n + 2:8 * n + 3], st[0:rows, 40:41],
                                   ALU.pow).then_inc(s[f"y{n}_rstd"], 1)

            def add_bias(i):
                pool.wait_ge(s["x1_ready"], i + 1)
                wait(pool, "y2_ready", i)
                if isinstance(i, int) and i == 0:
                    pool.wait_ge(s["bx_ready"], 1)
                pool.tensor_tensor(x1b[:, :], x1[:, :], b_x[:, :], ALU.add).then_inc(s["x1b_ready"], 1)

            copy_x(0)
            pool.iota(iota_i[:, 0:P], pattern=[[1, P]], base=0, channel_multiplier=-1).then_inc(s["ones_ready"], 1)
            pool.iota(iota_i[:, P:2 * P], pattern=[[1, P]], base=0, channel_multiplier=0).then_inc(s["ones_ready"], 1)
            pool.iota(iota_i[:, 2 * P:2 * P + B], pattern=[[S, B]], base=0, channel_multiplier=1).then_inc(s["ones_ready"], 1)
            pool.memset(st[:, 40:41], -0.5).then_inc(s["ones_ready"], 1)
            pool.memset(ones[:, :], 1.0).then_inc(s["ones_ready"], 1)
            pool.memset(ones3[:, :], 0.0).then_inc(s["ident_ready"], 1)
            pool.memset(ones16[:, :], 1.0).then_inc(s["ones_ready"], 1)
            pool.wait_ge(s["ident_ready"], 3)
            pool.memset(ones3[0:3, :], 1.0).then_inc(s["ones_ready"], 1)
            pool.wait_ge(s["ones_ready"], 7)
            pool.affine_select(out=low16[:, :], in_=ones16[:, :], compare_op=ALU.is_gt, fill=0.0, base=0,
                               pattern=[[1, P]], channel_multiplier=-1).then_inc(s["ones_ready"], 1)
            pool.wait_ge(s["alibi_flat"], 1)
            pool.affine_select(out=alibi[:, :], in_=alibi[:, :], compare_op=ALU.is_ge, fill=MASKED, base=0,
                               pattern=[[-1, S]], channel_multiplier=1).then_inc(s["alibi_ready"], 1)
            copy_ctx(0)
            rstd(1, 0, S)
            copy_x(1)
            pool.memset(bias_rows[:, :].bitcast(F32), 0.0).then_inc(s["bias_zeroed"], 1)
            pool.wait_ge(s["bias_split"], 1)
            pool.dma_start(bias_parts.rearrange("n e f -> e n f"), bpart[:, :, :]).then_inc(s["bias_stored"], 16)
            pool.wait_ge(s["bias_stored"], 16)
            pool.wait_ge(s["bias_zeroed"], 1)
            pool.dma_start(bias_rows[0:3, :], bias_parts.rearrange("n e f -> n (e f)")).then_inc(s["bias_in"], 16)
            add_bias(0)
            rstd(1, 1, S)
            copy_x(2)
            copy_ctx(1)
            rstd(2, 0, S)
            add_bias(1)
            with pool.Fori(2, B - 1) as i:
                rstd(1, i, S)
                copy_x(i + 1)
                copy_ctx(i)
                rstd(2, i - 1, S)
                add_bias(i)
            rstd(1, B - 1, S)
            copy_ctx(B - 1)
            rstd(2, B - 2, S)
            add_bias(B - 1)
            rstd(2, B - 1, S)

            last_row = pool.to_reg(N - 1)

            def gather(u, k):
                pool.wait_ge(idx_ready[u], k + 1)
                waited(pool)
                pool.indirect_dma_start(xg[u], None, x2_rows, bass.IndirectOffsetOnAxis(ap=idx_in[u][:, :].bitcast(U32), axis=0),
                                        bounds_check=last_row, oob_is_err=False).then_inc(gathered[u], 16)

            pool.wait_ge(s["x2_stored"], 16 * B)
            gather(0, 0)
            gather(1, 0)
            with pool.Fori(0, SLOTS // 2) as t:
                for u in range(2):
                    pool.wait_ge(s["y3_stats"], 2 * t + u + 1)
                    pool.tensor_tensor(st[:, 26:27], st[:, 26:27], st[:, 40:41], ALU.pow).then_inc(s["y3_rstd"], 1)
                    gather(u, t + 1)
                    pool.wait_ge(s["o_ready"], 2 * t + u + 1)
                    pool.wait_ge(oidx_ready[u], t + 1)
                    waited(pool)
                    pool.indirect_dma_start(out.rearrange("b s d -> (b s) d"),
                                            bass.IndirectOffsetOnAxis(ap=idx_out[u][:, :].bitcast(U32), axis=0),
                                            y3n[u], None, bounds_check=last_row, oob_is_err=False).then_inc(scattered[u], 16)
            for u in range(2):
                pool.wait_ge(scattered[u], 16 * (SLOTS // 2))
                pool.wait_ge(gathered[u], 16 * (SLOTS // 2 + 1))

        @block.scalar
        def _(act):
            def load_expert(e):
                act.dma_start(w_ex[:, bass.ds(e * WE, WE // 2)].rearrange("p (c f) -> p c f", c=DC),
                              w1[bass.ds(e, 1), :, :].rearrange("o (c p) f -> p (o c) f", p=P)).then_inc(s["experts_in"], 16)
                act.dma_start(w_ex[:, bass.ds(e * WE + WE // 2, WE // 2)].rearrange("p (c d) -> p c d", c=FC),
                              w2[bass.ds(e, 1), :, :].rearrange("o (c p) d -> p (o c) d", p=P)).then_inc(s["experts_in"], 16)

            def copy(dst, src, scale=1.0):
                return act.activation(dst, src, ACT.Copy, scale=scale)

            def body(i, do_s, do_c, do_g):
                c, g = i - 1, i - 2
                if do_s:
                    act.wait_ge(s["xT_psum"], i + 1)
                    copy(xT[:, :, :], cols2(0)).then_inc(s["xT_ready"], 1)
                if do_c:
                    act.wait_ge(s["cT_psum"], c + 1)
                    for d in range(DC):
                        copy(cT[:, d, :], bank[4 + d][:, 0:SK]).then_inc(s["cT_ready"], 1)
                if do_s:
                    act.wait_ge(s["gT_psum"], i + 1)
                    copy(gT[:, :, :], cols2(1), SCALE).then_inc(s["gT_ready"], 1)
                if do_c:
                    act.wait_ge(s["x1T_psum"], c + 1)
                    copy(x1T[:, :, :], cols2(2)).then_inc(s["x1T_ready"], 1)
                if do_s:
                    act.wait_ge(s["sc_max"], i + 1)
                    wait(act, "pT_psum", i)
                    act.activation(pr[:, :], sc[:, :], ACT.Exp, bias=st[0:S, 0:1], accum_out=st[0:S, 1:2]).then_inc(s["p_ready"], 1)
                if do_c:
                    act.wait_ge(s["rT_psum"], c + 1)
                    for d in range(DC):
                        act.activation(rT[:, d, :], cols2(3)[:, d, :], ACT.Identity, bias=c_x[:, d:d + 1]).then_inc(s["rT_ready"], 1)
                if do_g:
                    act.wait_ge(s["x2T_psum"], g + 1)
                    copy(x2T[:, :, :], cols2(7)).then_inc(s["x2T_ready"], 1)
                if do_s:
                    act.wait_ge(s["pT_psum"], i + 1)
                    copy(pT[:, :], bank[1][0:S, 0:S]).then_inc(s["pT_ready"], 1)
                if do_c:
                    act.wait_ge(s["sc2_max"], c + 1)
                    act.activation(pc[:, :], bank[2][0:S, 0:SK], ACT.Exp, bias=st[0:S, 2:3], accum_out=st[0:S, 3:4]).then_inc(s["pc_ready"], 1)
                    act.wait_ge(s["pcT_psum"], c + 1)
                    copy(pcT[:, :, :], bank[6][0:SP_, 0:KC * S].rearrange("p (c n) -> p c n", c=KC)).then_inc(s["pcT_ready"], 1)
                    act.wait_ge(s["ccT_psum"], c + 1)
                    copy(ccT[:, :, :], cols2(3)).then_inc(s["ccT_ready"], 1)

            load_expert(0)
            body(0, True, False, False)
            act.wait_ge(s["wvT_psum"], 1)
            copy(wvT[:, :, :], bank[4][:, :].rearrange("p (c d) -> p c d", c=DC)).then_inc(s["wvT_ready"], 1)
            act.wait_ge(s["woT_psum"], 1)
            copy(woT, bank[5][:, :].rearrange("p (c d) -> p c d", c=DC)).then_inc(s["woT_ready"], 1)
            act.wait_ge(s["a_psum"], 1)
            copy(a_x[:, :, :], bank[6][:, :].rearrange("p (c d) -> p c d", c=DC), SCALE).then_inc(s["a_ready"], 1)
            act.wait_ge(s["m_psum"], 1)
            copy(m_x[:, :, :], bank[7][:, :].rearrange("p (c d) -> p c d", c=DC)).then_inc(s["m_ready"], 1)
            act.wait_ge(s["gwT_psum"], 1)
            copy(gwT[:, :, :], bank[4][:, 0:DC * E].rearrange("p (c d) -> p c d", c=DC)).then_inc(s["gwT_ready"], 1)
            act.wait_ge(s["c_psum"], 1)
            copy(c_x[:, :], bank[5][:, 0:DC], SCALE).then_inc(s["c_ready"], 1)
            act.wait_ge(s["c_ready"], 1)
            act.wait_ge(s["bx_psum"], 1)
            copy(b_x[:, :], bank[6][0:S, 0:D]).then_inc(s["bx_ready"], 1)
            body(1, True, True, False)
            with act.Fori(2, B) as i:
                load_expert(i - 1)
                body(i, True, True, True)
            body(B, False, True, True)
            body(B + 1, False, False, True)
            act.wait_ge(s["out2_psum"], B)
            act.wait_ge(s["x2_ready"], B)
            load_expert(E - 1)

            def xg_evacuated(n):
                act.wait_ge(s["xgT_psum"], n + 1)
                copy(xgT, cols2(6, P)).then_inc(s["xgT_ready"], 1)

            xg_evacuated(0)
            with act.Fori(0, SLOTS // 2) as t:
                for u in range(2):
                    n = 2 * t + u
                    act.wait_ge(s["h0_psum"], n + 1)
                    act.activation(hid[:, 0:FH], bank[0][:, :], ACT.Relu).then_inc(s["h0_ready"], 1)
                    act.wait_ge(s["h1_psum"], n + 1)
                    act.activation(hid[:, FH:F], bank[1][:, :], ACT.Relu).then_inc(s["h1_ready"], 1)
                    xg_evacuated(n + 1)
                    act.wait_ge(s["hT1_psum"], n + 1)
                    copy(hidT[:, FC // 2:FC, :], bank[3][:, :].rearrange("p (c n) -> p c n", c=FC // 2)).then_inc(s["hT1_ready"], 1)

        @block.vector
        def _(dve):
            done = [0]

            def link(ins):
                done[0] += 1
                ins.then_inc(s["route"], 1)
                dve.wait_ge(s["route"], done[0])

            dve.wait_ge(s["ones_ready"], 8)
            dve.wait_ge(s["small_in"], 16 * 9)
            link(dve.tensor_copy(sc[:, :], iota_i[0:S, 0:S]))
            dve.tensor_scalar(alibi[:, :], sc[:, :], slope_c[:, 0:1], None, ALU.mult).then_inc(s["alibi_flat"], 1)
            dve.tensor_tensor(gb[:, :], gb_raw[:, 0, :], gb_raw[:, 1, :], ALU.add).then_inc(s["logit_ready"], 1)
            dve.tensor_copy(bv_wide[:, :, :], bv_col[:, :].unsqueeze(2).to_broadcast([P, DC, S])).then_inc(s["wide_ready"], 1)

            def ln_stats(n, y, rows, k):
                part = st[0:rows, 38 + 6 * n:44 + 6 * n]
                dve.wait_ge(s[f"y{n}_ready"], k + 1 + (n == 3))
                dve.bn_stats(part, y).then_inc(s[f"y{n}_bn"], 1)
                dve.wait_ge(s[f"y{n}_bn"], k + 1)
                waited(dve)
                dve.bn_aggr(st[0:rows, 8 * n + 1:8 * n + 3], part).then_inc(s[f"y{n}_agg"], 1)
                dve.wait_ge(s[f"y{n}_agg"], k + 1)
                dve.tensor_scalar(st[0:rows, 8 * n + 2:8 * n + 3], st[0:rows, 8 * n + 2:8 * n + 3], EPS, None,
                                  ALU.add).then_inc(s[f"y{n}_stats"], 1)

            def ln_apply(n, dst, y, rows, k):
                dve.wait_ge(s[f"y{n}_rstd"], k + 1)
                return dve.tensor_scalar(dst, y, st[0:rows, 8 * n + 1:8 * n + 2], st[0:rows, 8 * n + 2:8 * n + 3],
                                         ALU.subtract, ALU.mult)

            def body(i, do_s, do_c, do_g):
                c, g = i - 1, i - 2
                if do_s:
                    dve.wait_ge(s["sc_psum"], i + 1)
                    if isinstance(i, int) and i == 0:
                        dve.wait_ge(s["alibi_ready"], 1)
                    dve.tensor_tensor(sc[:, :], bank[0][0:S, 0:S], alibi[:, :], ALU.add).then_inc(s["sc_biased"], 1)
                    dve.wait_ge(s["sc_biased"], i + 1)
                    dve.tensor_reduce(st[0:S, 0:1], sc[:, :], AX.X, ALU.max, negate=True).then_inc(s["sc_max"], 1)
                if do_c:
                    dve.wait_ge(s["sc2_psum"], c + 1)
                    dve.tensor_reduce(st[0:S, 2:3], bank[2][0:S, 0:SK], AX.X, ALU.max, negate=True).then_inc(s["sc2_max"], 1)
                if do_s:
                    dve.wait_ge(s["p_ready"], i + 1)
                    dve.reciprocal(st[0:S, 4:5], st[0:S, 1:2]).then_inc(s["p_inv"], 1)
                    dve.wait_ge(s["uT_psum"], i + 1)
                    dve.tensor_copy(uT[:, :, :], cols2(0)).then_inc(s["uT_ready"], 1)
                if do_c:
                    dve.wait_ge(s["pc_ready"], c + 1)
                    dve.reciprocal(st[0:S, 5:6], st[0:S, 3:4]).then_inc(s["pc_inv"], 1)
                if do_g:
                    dve.wait_ge(s["gate_psum"], g + 1)
                    dve.wait_ge(s["logit_ready"], 1)
                    dve.tensor_tensor(logit[:, bass.ds(g, 1), :].rearrange("p o e -> p (o e)"), bank[7][0:S, 0:E],
                                      gb[:, :], ALU.add).then_inc(s["logit_ready"], 1)
                if do_s:
                    dve.wait_ge(s["out1_psum"], i + 1)
                    dve.wait_ge(s["p_inv"], i + 1)
                    dve.scalar_tensor_tensor(y1[:, :], bank[1][0:S, 0:D], st[0:S, 4:5], xw[:, :],
                                             ALU.mult, ALU.add).then_inc(s["y1_ready"], 1)
                    ln_stats(1, y1[:, :], S, i)
                if do_c:
                    dve.wait_ge(s["out2_psum"], c + 1)
                    dve.wait_ge(s["pc_inv"], c + 1)
                    dve.wait_ge(s["x1b_ready"], c + 1)
                    dve.scalar_tensor_tensor(y2[:, :], bank[2][0:S, 0:D], st[0:S, 5:6], x1b[:, :],
                                             ALU.mult, ALU.add).then_inc(s["y2_ready"], 1)
                    ln_stats(2, y2[:, :], S, c)
                if do_s:
                    ln_apply(1, x1[:, :], y1[:, :], S, i).then_inc(s["x1_ready"], 1)
                if do_c:
                    wait(dve, "x2_stored", 16 * c)
                    ln_apply(2, x2[:, :], y2[:, :], S, c).then_inc(s["x2_ready"], 1)

            body(0, True, False, False)
            hi, mid, low = (bpart[:, n, :] for n in range(3))
            rest = shared[0:E, 3072:3072 + BR]
            link(dve.tensor_copy(hi, bst))
            link(dve.tensor_tensor(rest, bst, hi, ALU.subtract))
            link(dve.tensor_copy(mid, rest))
            link(dve.tensor_tensor(rest, rest, mid, ALU.subtract))
            link(dve.tensor_copy(low, rest))
            dve.tensor_copy(st[0:1, 62:63], st[0:1, 4:5]).then_inc(s["bias_split"], 1)
            body(1, True, True, False)
            with dve.Fori(2, B) as i:
                body(i, True, True, True)
            body(B, False, True, True)
            body(B + 1, False, False, True)

            at = [0]

            def room(*shape):
                n = 1
                for d in shape:
                    n *= d
                v = rt[:, at[0]:at[0] + n]
                at[0] += n
                if len(shape) == 2:
                    v = v.rearrange("p (a b) -> p a b", b=shape[1])
                if len(shape) == 3:
                    v = v.rearrange("p (a b c) -> p a b c", b=shape[1], c=shape[2])
                return v

            num = room(P)
            token = room(B)
            back = room(E)
            dve.wait_ge(s["bias_stored"], 16)
            link(dve.tensor_copy(num, iota_i[0:S, P:2 * P]))
            link(dve.tensor_copy(token, iota_i[0:S, 2 * P:2 * P + B]))
            link(dve.tensor_scalar(back, num[:, 0:E], -1.0, float(E), ALU.mult, ALU.add))
            top = room(B)
            hot = room(B, E)
            pick = room(B)
            dve.wait_ge(s["logit_ready"], B + 1)
            link(dve.tensor_reduce(top, logit[:, :, :], AX.X, ALU.max))
            link(dve.tensor_tensor(hot, logit[:, :, :], top.unsqueeze(2).to_broadcast([S, B, E]), ALU.is_equal))
            link(dve.tensor_tensor(hot, hot, back.unsqueeze(1).to_broadcast([S, B, E]), ALU.mult))
            link(dve.tensor_reduce(pick, hot, AX.X, ALU.max))
            link(dve.tensor_tensor(hot, pick.unsqueeze(2).to_broadcast([S, B, E]),
                                   back.unsqueeze(1).to_broadcast([S, B, E]), ALU.is_equal))
            link(dve.tensor_copy(oh16[:, :, :], hot))
            count = room(E)
            link(dve.tensor_reduce(count, hot.rearrange("p b e -> p e b"), AX.X, ALU.add))
            dve.tensor_copy(ohs16[:, :], count).then_inc(s["hot_ready"], 1)
            dve.wait_ge(s["rank_psum"], 1)
            bound = room(TILES)
            more = room(E, TILES)
            tiles = room(E)
            before = room(E, E)
            first = room(E)
            link(dve.tensor_scalar(bound, num[:, 0:TILES], float(P), None, ALU.mult))
            link(dve.tensor_copy(count, bank[1][0:S, 0:E]))
            link(dve.tensor_tensor(more, count.unsqueeze(2).to_broadcast([S, E, TILES]),
                                   bound.unsqueeze(1).to_broadcast([S, E, TILES]), ALU.is_gt))
            link(dve.tensor_reduce(tiles, more, AX.X, ALU.add))
            link(dve.tensor_tensor(before, num[:, 0:E].unsqueeze(1).to_broadcast([S, E, E]),
                                   num[:, 0:E].unsqueeze(2).to_broadcast([S, E, E]), ALU.is_lt))
            link(dve.tensor_tensor(before, before, tiles.unsqueeze(1).to_broadcast([S, E, E]), ALU.mult))
            link(dve.tensor_reduce(first, before, AX.X, ALU.add))
            starts = room(COLS, E - 1)
            owner = room(COLS)
            link(dve.tensor_tensor(starts, num[:, 0:COLS].unsqueeze(2).to_broadcast([S, COLS, E - 1]),
                                   first[:, 1:E].unsqueeze(1).to_broadcast([S, COLS, E - 1]), ALU.is_ge))
            link(dve.tensor_reduce(owner, starts, AX.X, ALU.add))
            dve.tensor_copy(slot_expert[:, :], owner[0:1, :]).then_inc(s["used_ready"], 1)
            rank = room(B, E)
            mine = room(B)
            base = room(B)
            over = room(B, TILES - 1)
            tile = room(B)
            link(dve.tensor_tensor(rank, hot, bank[0][0:S, 0:B * E].rearrange("p (b e) -> p b e", e=E), ALU.mult))
            link(dve.tensor_reduce(mine, rank, AX.X, ALU.add))
            link(dve.tensor_tensor(rank, hot, first.unsqueeze(1).to_broadcast([S, B, E]), ALU.mult))
            link(dve.tensor_reduce(base, rank, AX.X, ALU.add))
            link(dve.tensor_tensor(over, mine.unsqueeze(2).to_broadcast([S, B, TILES - 1]),
                                   bound[:, 1:TILES].unsqueeze(1).to_broadcast([S, B, TILES - 1]), ALU.is_ge))
            link(dve.tensor_reduce(tile, over, AX.X, ALU.add))
            link(dve.tensor_tensor(base, base, tile, ALU.add))
            link(dve.scalar_tensor_tensor(mine, tile, -float(P), mine, ALU.mult, ALU.add))
            link(dve.tensor_tensor(place16[:, :, :], num.unsqueeze(1).to_broadcast([S, B, P]),
                                   mine.unsqueeze(2).to_broadcast([S, B, P]), ALU.is_equal))
            link(dve.tensor_tensor(slot16[:, :, 1, :], num[:, 0:COLS].unsqueeze(1).to_broadcast([S, B, COLS]),
                                   base.unsqueeze(2).to_broadcast([S, B, COLS]), ALU.is_equal))
            dve.tensor_tensor(slot16[:, :, 0, :], slot16[:, :, 1, :],
                              token.unsqueeze(2).to_broadcast([S, B, COLS]), ALU.mult).then_inc(s["table16_ready"], 1)
            dve.wait_ge(s["table_psum"], 1)
            unused = hidT[:, 0, 0:COLS]
            link(dve.tensor_scalar(unused, bank[2][:, COLS:2 * COLS], -float(DROP), float(DROP), ALU.mult, ALU.add))
            link(dve.tensor_copy(row_in[:, :], bank[2][:, 0:COLS]))
            link(dve.tensor_tensor(row_out[:, :], bank[2][:, 0:COLS], unused, ALU.add))
            for u in range(2):
                dve.tensor_copy(idx_in[u][:, :], row_in[:, u:u + 1]).then_inc(idx_ready[u], 1)

            dve.sem_inc(s["y3_ready"], 1)
            def slot_pair(t):
                for u in range(2):
                    n = 2 * t + u
                    dve.wait_ge(gathered[u], 16 * (t + 1))
                    dve.tensor_copy(idx_in[u][:, :], row_in[:, bass.ds(n + 2, 1)]).then_inc(idx_ready[u], 1)
                    if not (isinstance(t, int) and t == 0):
                        dve.wait_ge(scattered[u], 16 * t)
                    dve.tensor_copy(idx_out[u][:, :], row_out[:, bass.ds(n, 1)]).then_inc(oidx_ready[u], 1)
                    dve.wait_ge(s["hT0_psum"], n + 1)
                    dve.tensor_copy(hidT[:, 0:FC // 2, :], bank[2][:, :].rearrange("p (c n) -> p c n", c=FC // 2)).then_inc(s["hT0_ready"], 1)
                    dve.wait_ge(s["y3_psum"], n + 1)
                    dve.tensor_tensor(y3, bank[4][:, 0:D], xg[u], ALU.add).then_inc(s["y3_ready"], 1)
                    ln_stats(3, y3, P, n)
                    ln_apply(3, y3n[u], y3, P, n).then_inc(s["o_ready"], 1)

            slot_pair(0)
            with dve.Fori(1, SLOTS // 2) as t:
                slot_pair(t)

        @block.tensor
        def _(pe):
            def mm(dst, lhsT, rhs, k, last):
                return pe.matmul(dst, lhsT, rhs, start=(k == 0), stop=(k == last))

            def project(dst, weights, act_T):
                for e in range(DC):
                    for d in range(DC):
                        last = mm(dst[:, e, :], weights[:, d, e * P:(e + 1) * P], act_T[:, d, :], d, DC - 1)
                return last

            def flip(b, src, rows):
                for d in range(DC):
                    last = pe.transpose(cols2(b, rows)[:, d, :], src[:, d * P:(d + 1) * P], ident[0:rows, 0:rows])
                return last

            def flip_weights(b, src):
                dst = bank[b][:, :].rearrange("p (c d) -> p c d", c=DC)
                for d in range(DC):
                    for e in range(DC):
                        last = pe.transpose(dst[:, d, e * P:(e + 1) * P], src[:, e, d * P:(d + 1) * P], ident[:, :])
                return last

            def body(i, do_s, do_c, do_g):
                c, g = i - 1, i - 2
                if do_s:
                    pe.wait_ge(s["x_copied"], i + 1)
                    flip(0, xw, S).then_inc(s["xT_psum"], 1)
                if do_c:
                    pe.wait_ge(s["c_copied"], c + 1)
                    for d in range(DC):
                        for k in range(KC):
                            last = pe.transpose(bank[4 + d][:, k * SP_:(k + 1) * SP_], cw[:, k, d * P:(d + 1) * P], ident[0:SP_, 0:SP_])
                    last.then_inc(s["cT_psum"], 1)
                if do_s:
                    pe.wait_ge(s["xT_ready"], i + 1)
                    wait(pe, "y1_ready", i)
                    project(cols2(1), wqk_s, xT).then_inc(s["gT_psum"], 1)
                if do_c:
                    pe.wait_ge(s["x1_ready"], c + 1)
                    wait(pe, "y2_ready", c)
                    flip(2, x1, S).then_inc(s["x1T_psum"], 1)
                if do_s:
                    pe.wait_ge(s["gT_ready"], i + 1)
                    for d in range(DC):
                        last = mm(bank[0][0:S, 0:S], gT[:, d, :], xT[:, d, :], d, DC - 1)
                    last.then_inc(s["sc_psum"], 1)
                if do_c:
                    pe.wait_ge(s["x1T_ready"], c + 1)
                    project(cols2(3), a_x, x1T).then_inc(s["rT_psum"], 1)
                if do_g:
                    pe.wait_ge(s["x2_ready"], g + 1)
                    wait(pe, "logit_ready", g + 1)
                    flip(7, x2, S).then_inc(s["x2T_psum"], 1)
                if do_c:
                    pe.wait_ge(s["rT_ready"], DC * (c + 1))
                    pe.wait_ge(s["cT_ready"], DC * (c + 1))
                    for d in range(DC):
                        last = mm(bank[2][0:S, 0:SK], rT[:, d, :], cT[:, d, :], d, DC - 1)
                    last.then_inc(s["sc2_psum"], 1)
                if do_s:
                    pe.wait_ge(s["p_ready"], i + 1)
                    pe.transpose(bank[1][0:S, 0:S], pr[:, :], ident[0:S, 0:S]).then_inc(s["pT_psum"], 1)
                    pe.wait_ge(s["pT_ready"], i + 1)
                    for d in range(DC):
                        last = mm(cols2(0)[:, d, :], xw[:, d * P:(d + 1) * P], pT[:, :], 0, 0)
                    last.then_inc(s["uT_psum"], 1)
                if do_c:
                    pe.wait_ge(s["pc_ready"], c + 1)
                    for k in range(KC):
                        last = pe.transpose(bank[6][0:SP_, k * S:(k + 1) * S], pc[:, k * SP_:(k + 1) * SP_], ident[0:S, 0:S])
                    last.then_inc(s["pcT_psum"], 1)
                if do_g:
                    pe.wait_ge(s["x2T_ready"], g + 1)
                    for d in range(DC):
                        last = mm(bank[7][0:S, 0:E], x2T[:, d, :], gwT[:, d, :], d, DC - 1)
                    last.then_inc(s["gate_psum"], 1)
                if do_c:
                    pe.wait_ge(s["pcT_ready"], c + 1)
                    for d in range(DC):
                        for k in range(KC):
                            last = mm(cols2(3)[:, d, :], cw[:, k, d * P:(d + 1) * P], pcT[:, k, :], k, KC - 1)
                    last.then_inc(s["ccT_psum"], 1)
                if do_s:
                    pe.wait_ge(s["uT_ready"], i + 1)
                    pe.wait_ge(s["wvT_ready"], 1)
                    for d in range(DC):
                        last = mm(bank[1][0:S, 0:D], uT[:, d, :], wvT[:, d, :], d, DC - 1)
                    last.then_inc(s["out1_psum"], 1)
                if do_c:
                    pe.wait_ge(s["ccT_ready"], c + 1)
                    for d in range(DC):
                        last = mm(bank[2][0:S, 0:D], ccT[:, d, :], m_x[:, d, :], d, DC - 1)
                    last.then_inc(s["out2_psum"], 1)

            pe.wait_ge(s["ident_ready"], 3)
            pe.wait_ge(s["weights_in"], 16 * 6)
            flip_weights(4, raw_wv).then_inc(s["wvT_psum"], 1)
            body(0, True, False, False)
            flip_weights(5, raw_wo).then_inc(s["woT_psum"], 1)
            pe.wait_ge(s["small_in"], 16 * 9)
            for d in range(DC):
                last = pe.transpose(bank[4][:, d * E:(d + 1) * E], gw_raw[:, d * P:(d + 1) * P], ident[0:E, 0:E])
            last.then_inc(s["gwT_psum"], 1)
            for d in range(DC):
                for e in range(DC):
                    last = mm(bank[6][:, d * D:(d + 1) * D], raw_wq[:, e, d * P:(d + 1) * P], raw_wk[:, e, :], e, DC - 1)
            last.then_inc(s["a_psum"], 1)
            pe.wait_ge(s["woT_ready"], 1)
            for d in range(DC):
                for e in range(DC):
                    last = mm(bank[7][:, d * D:(d + 1) * D], raw_xv[:, e, d * P:(d + 1) * P], woT[:, e, :], e, DC - 1)
            last.then_inc(s["m_psum"], 1)
            for d in range(DC):
                for e in range(DC):
                    last = mm(bank[5][:, d:d + 1], raw_wk[:, e, d * P:(d + 1) * P], bq_col[:, e:e + 1], e, DC - 1)
            last.then_inc(s["c_psum"], 1)
            pe.wait_ge(s["a_ready"], 1)
            pe.wait_ge(s["wide_ready"], 1)
            pe.wait_ge(s["ones_ready"], 8)
            for e in range(DC):
                mm(bank[6][0:S, 0:D], bv_wide[:, e, :], woT[:, e, :], e, DC)
            mm(bank[6][0:S, 0:D], ones[0:1, 0:S], bo_row[:, :], DC, DC).then_inc(s["bx_psum"], 1)
            for name in ("m_ready", "gwT_ready", "c_ready", "bx_ready"):
                pe.wait_ge(s[name], 1)
            body(1, True, True, False)
            with pe.Fori(2, B) as i:
                body(i, True, True, True)
            body(B, False, True, True)
            body(B + 1, False, False, True)

            pe.wait_ge(s["hot_ready"], 1)
            for b in range(B - 1):
                pe.matmul(bank[0][:, (b + 1) * E:B * E], ones16[:, :],
                          oh16[:, b:b + 1, :].to_broadcast([S, B - 1 - b, E]), start=(b == 0), stop=False, skip_group_check=True)
            pe.matmul(bank[0][:, 0:B * E], low16[:, :], oh16[:, :, :].rearrange("p b e -> p (b e)"),
                      start=False, stop=True, skip_group_check=True)
            pe.matmul(bank[1][:, 0:E], ones16[:, :], ohs16[:, :], start=True, stop=True).then_inc(s["rank_psum"], 1)
            pe.wait_ge(s["table16_ready"], 1)
            for b in range(B):
                last = mm(bank[2][:, 0:2 * COLS], place16[:, b, :], slot16[:, b, :, :].rearrange("p t c -> p (t c)"), b, B - 1)
            last.then_inc(s["table_psum"], 1)

            def flip_rows(u, k):
                pe.wait_ge(gathered[u], 16 * (k + 1))
                flip(6, xg[u], P).then_inc(s["xgT_psum"], 1)

            flip_rows(0, 0)
            pe.wait_ge(s["used_ready"], 1)
            pe.wait_ge(s["bias_in"], 16)
            pe.wait_ge(s["experts_in"], 32 * E)
            with pe.Fori(0, SLOTS // 2) as t:
                for u in range(2):
                    n = 2 * t + u
                    e = pe.value_load(slot_expert[0:1, bass.ds(n, 1)], min_val=0, max_val=E - 1)
                    pe.wait_ge(s["xgT_ready"], n + 1)
                    for h in range(2):
                        for d in range(DC):
                            mm(bank[h][:, :], xgT[:, d, :], w_ex[:, bass.ds(e * WE + d * F + h * FH, FH)], d, DC)
                        mm(bank[h][:, :], ones3[:, :], bias_rows[:, bass.ds(e * BR + h * FH, FH)], DC, DC).then_inc(s[f"h{h}_psum"], 1)
                    flip_rows(1 - u, t + u)
                    for h in range(2):
                        pe.wait_ge(s[f"h{h}_ready"], n + 1)
                        for k in range(FC // 2):
                            f = h * FC // 2 + k
                            last = pe.transpose(bank[2 + h][:, k * P:(k + 1) * P], hid[:, f * P:(f + 1) * P], ident[:, :])
                        last.then_inc(s[f"hT{h}_psum"], 1)
                    pe.wait_ge(s["y3_ready"], n + 1)
                    for h in range(2):
                        pe.wait_ge(s[f"hT{h}_ready"], n + 1)
                        for k in range(FC // 2):
                            f = h * FC // 2 + k
                            mm(bank[4][:, 0:D], hidT[:, f, :], w_ex[:, bass.ds(e * WE + DC * F + f * D, D)], f, FC)
                    mm(bank[4][:, 0:D], ones3[:, :], bias_rows[:, bass.ds(e * BR + F, D)], FC, FC).then_inc(s["y3_psum"], 1)


_INS = ["x", "ctx_1024", "L0_attn_W_qk", "L0_attn_W_v", "L0_attn_alibi_slope", "L0_xattn_Wk", "L0_xattn_Wv",
        "L0_xattn_bv", "L0_xattn_Wq", "L0_xattn_bq", "L0_xattn_Wo", "L0_xattn_bo", "L0_ffn_gate_w", "L0_ffn_gate_b",
        "L0_ffn_expert_bias", "L0_ffn_w1", "L0_ffn_b1", "L0_ffn_w2", "L0_ffn_b2"]


def kernel(**inputs):
    import numpy as np
    import concourse.bacc as bacc
    from concourse.bass_utils import run_bass_kernel_spmd

    nc = bacc.Bacc("TRN2", target_bir_lowering=False, num_devices=1)
    arrays, args = {}, []
    for name in _INS:
        a = np.ascontiguousarray(inputs[name])
        arrays[f"in_{name}"] = a
        args.append(nc.dram_tensor(f"in_{name}", a.shape, mybir.dt.from_np(a.dtype), kind="ExternalInput").ap())
    out = nc.dram_tensor("out_0", inputs["x"].shape, F32, kind="ExternalOutput").ap()
    decoder_layer(nc, *args, out)
    r = run_bass_kernel_spmd(nc, [arrays], core_ids=[0])
    return r.results[0]["out_0"]
```

```python
from contextlib import ExitStack

import concourse.bass as bass
from concourse import mybir

F32 = mybir.dt.float32
BF16 = mybir.dt.bfloat16
F16 = mybir.dt.float16
I32 = mybir.dt.int32
U32 = mybir.dt.uint32
ALU = mybir.AluOpType
ACT = mybir.ActivationFunctionType
AX = mybir.AxisListType

P = 128
MASKED = -1.0e30
EPS = 1e-5
DROP = 4096


def decoder_layer(nc, x, ctx_in, w_qk, w_v, slope, wk, w_xv, bv, wq, bq, wo, bo,
                  gate_w, gate_b, expert_bias, w1, b1, w2, b2, out):
    B, S, D = x.shape
    SK = ctx_in.shape[1]
    E, _, F = w1.shape
    DC = D // P
    KC = 3
    SP_ = SK // KC
    FC = F // P
    N = B * S
    TILES = -(-N // P)
    SLOTS = TILES + E - 1
    COLS = SLOTS + 2
    WE = 2 * DC * F
    QW = WE // 4
    QF = F // 4
    SCALE = float(D) ** -0.5
    assert S <= P and SP_ * KC == SK and SP_ <= P and DC == 2 and FC * D == DC * F

    with ExitStack() as stack:
        def sb(name, shape, dt=F32):
            return stack.enter_context(nc.sbuf_tensor(name, shape, dt))

        def sem(name):
            return stack.enter_context(nc.semaphore(name))

        x2_rows = nc.dram_tensor("x2_rows", [N, D], F32, kind="Internal").ap()
        b2_parts = nc.dram_tensor("b2_parts", [3, E, D], BF16, kind="Internal").ap()

        w_hi = sb("w_hi", [P, E * WE], F16)
        w_lo = sb("w_lo", [P, E * WE], BF16)
        b2_rows = sb("b2_rows", [P, E * D], BF16)
        b1T = sb("b1T", [P, E * FC])
        ident = sb("ident", [P, P])
        ones = sb("ones", [P, P])
        ones3 = sb("ones3", [P, P], BF16)
        alibi = sb("alibi", [S, S])
        num = sb("num", [S, P])
        num16 = sb("num16", [S, P], F16)
        iota_i = sb("iota_i", [P, 2 * P + B], I32)
        wqk_s = sb("wqk_s", [P, DC, D])
        wvT = sb("wvT", [P, DC, D])
        a_x = sb("a_x", [P, DC, D])
        m_x = sb("m_x", [P, DC, D])
        c_x = sb("c_x", [P, DC])
        b_x = sb("b_x", [S, D])
        gwT = sb("gwT", [P, DC, E])
        gb = sb("gb", [S, E])
        stage = sb("stage", [P, WE])
        raw = stage[:, 0:5 * DC * D].rearrange("p (n c d) -> p n c d", n=5, c=DC)
        raw_wv, raw_wo, raw_wq, raw_wk, raw_xv = (raw[:, n] for n in range(5))
        woT = raw_wq
        b1_raw = sb("b1_raw", [E * FC, P])
        b2_raw = sb("b2_raw", [E, D])
        b2_split = sb("b2_split", [E, 3, D], BF16)
        gw_raw = sb("gw_raw", [E, D])
        gb_raw = sb("gb_raw", [S, 2, E])
        bq_col = sb("bq_col", [P, DC])
        bv_col = sb("bv_col", [P, DC])
        bv_wide = sb("bv_wide", [P, DC, S])
        bo_row = sb("bo_row", [1, D])
        slope_c = sb("slope_c", [S, 1])
        xw = [sb(f"xw{u}", [S, D]) for u in range(2)]
        sc = sb("sc", [S, S])
        pr = sb("pr", [S, S])
        pT = sb("pT", [S, S])
        y1 = sb("y1", [S, D])
        x1 = sb("x1", [S, D])
        x1b = [sb(f"x1b{u}", [S, D]) for u in range(2)]
        x2 = sb("x2", [S, D])
        x2T = sb("x2T", [P, DC, S])
        work = sb("work", [P, 5888])

        class Room:

            def __init__(self):
                self.at = 0

            def take(self, rows, *shape, dt=F32):
                n = 1
                for d in shape:
                    n *= d
                words = n if dt == F32 else n // 2
                v = work[0:rows, self.at:self.at + words]
                self.at += words
                assert self.at <= work.shape[1]
                if dt != F32:
                    v = v.bitcast(dt)
                if len(shape) == 2:
                    v = v.rearrange("p (a b) -> p a b", b=shape[1])
                if len(shape) == 3:
                    v = v.rearrange("p (a b c) -> p a b c", b=shape[1], c=shape[2])
                return v

        own = sb("cw_own", [SP_, KC, D])
        room = Room()
        cw = [own[:, :, :], room.take(SP_, KC, D)]
        x_all = room.take(S, B, D)
        xT = room.take(P, DC, S)
        gT = room.take(P, DC, S)
        uT = room.take(P, DC, S)
        x1T = room.take(P, DC, S)
        rT = room.take(P, DC, S)
        cT = room.take(P, DC, SK)
        pc = room.take(S, SK)
        pcT = room.take(SP_, KC, S)
        ccT = room.take(P, DC, S)
        y2 = room.take(S, D)
        st = sb("st", [P, 64])
        logit = sb("logit", [S, B, E])
        oh16 = sb("oh16", [S, B, E], BF16)
        low16 = sb("low16", [S, P], BF16)
        ones16 = sb("ones16", [S, P], BF16)
        row_in = sb("row_in", [P, COLS], I32)
        row_out = sb("row_out", [P, COLS], I32)
        slot_expert = sb("slot_expert", [1, COLS], I32)
        slots_used = sb("slots_used", [1, 2], I32)
        idx_in = [sb(f"idx_in{u}", [P, 1], I32) for u in range(2)]
        idx_out = [sb(f"idx_out{u}", [P, 1], I32) for u in range(2)]

        room = Room()
        place16 = room.take(S, B, P, dt=F16)
        slot16 = room.take(S, B, 2, COLS, dt=F16)
        hid = room.take(P, F)
        hid_hi = room.take(P, FC, P, dt=F16)
        hid_lo = room.take(P, FC, P, dt=BF16)
        xg = [room.take(P, D) for u in range(2)]
        xgT_hi = room.take(P, DC, P, dt=F16)
        xgT_lo = room.take(P, DC, P, dt=BF16)
        y3 = room.take(P, D)
        y3n_both = room.take(P, 2 * D)
        y3n = [y3n_both[:, 0:D], y3n_both[:, D:2 * D]]
        x_keep = room.take(P, D)

        bank = [stack.enter_context(nc.psum_tensor(f"bank{n}", [P, 512], F32)) for n in range(8)]

        def cols2(b, n=S):
            return bank[b][:, 0:DC * n].rearrange("p (c n) -> p c n", c=DC)

        names = """x0_in x_in xw_ready ctx_in0 ctx_in1 wqk_in wv_in
            slope_in a_in m_in gate_in b1_in b2_raw_in ident_ready ones_ready
            alibi_flat alibi_ready wide_ready tables_ready
            wvT_psum wvT_ready woT_psum woT_ready gwT_psum gwT_ready a_psum a_ready m_psum m_ready c_psum
            c_ready bx_psum bx_ready b1_ready b2_split b2_stored b2_in b2_zeroed
            stage_in0 stage_in1 stage_in2 stage_in3 hi_ready0 hi_ready1 hi_ready2 hi_ready3
            lo_ready0 lo_ready1 lo_ready2 lo_ready3
            xT_psum xT_ready gT_psum gT_ready sc_psum sc_biased sc_max p_ready p_inv pT_psum pT_ready
            uT_psum uT_ready out1_psum y1_ready y1_bn y1_agg y1_eps y1_rstd x1_ready x1b_ready
            x1T_psum x1T_ready rT_psum rT_ready cT_psum cT_ready sc2_psum sc2_max pc_ready pc_inv
            pcT_psum pcT_ready ccT_psum ccT_ready out2_psum y2_ready y2_bn y2_agg y2_eps y2_rstd x2_ready x2_stored
            x2T_psum x2T_ready gate_psum logit_ready
            route route2 hot_ready rank_psum table16_ready table_psum used_ready
            idx_ready0 idx_ready1 oidx_ready0 oidx_ready1 gathered0 gathered1 kept xgT_psum xgT_hi_ready xgT_lo_ready
            h0_psum h1_psum h2_psum h3_psum h0_ready h1_ready h2_ready h3_ready
            hi0_ready hi1_ready hi2_ready hi3_ready lo0_ready lo1_ready lo2_ready lo3_ready y3_psum y3_ready y3_bn y3_agg y3_eps y3_rstd o_ready
            scattered0 scattered1 passed""".split()
        s = {n: sem(n) for n in names}
        c_in = [s["ctx_in0"], s["ctx_in1"]]
        gathered = [s["gathered0"], s["gathered1"]]
        scattered = [s["scattered0"], s["scattered1"]]
        idx_ready = [s["idx_ready0"], s["idx_ready1"]]
        oidx_ready = [s["oidx_ready0"], s["oidx_ready1"]]

        def waited(e):
            e.sem_inc(s["passed"], 1)

        class Step:

            def __init__(self, t, u):
                self.t, self.u = t, u
                self.n = 2 * t + u
                self.a, self.b, self.c, self.d, self.g = (self.batch(k) for k in range(5))

            def batch(self, k):
                n = self.n - k
                return n if not isinstance(n, int) or 0 <= n < B else None

            def half(self, k):
                side = (self.u - k) % 2
                return side, self.t + (self.u - k - side) // 2

        STAGES = 5
        FIRST = 4
        assert FIRST + E == B + STAGES - 1

        def part(w, e, q):
            return w[:, bass.ds(e * WE + q * QW, QW)]

        def staged(q):
            return stage[:, q * QW:(q + 1) * QW]

        def has_expert(p):
            return not isinstance(p.n, int) or p.n >= FIRST

        FULL = -(-(STAGES - 1) // 2)

        def run_steps(e, step, between=None):
            for n in range(2 * FULL):
                if between:
                    between(n)
                step(Step(n // 2, n % 2))
            with e.Fori(FULL, B // 2) as t:
                for u in range(2):
                    step(Step(t, u))
            for n in range(B, B + STAGES - 1):
                step(Step(n // 2, n % 2))

        block = stack.enter_context(nc.Block())

        @block.sync
        def _(sp):
            def load_ctx(k, step):
                side, before = step.half(k)
                if not (isinstance(before, int) and before == 0):
                    sp.wait_ge(s["ccT_psum"], step.n - k - 1)
                sp.dma_start(cw[side].rearrange("p c d -> p (c d)") if side else cw[side][:, :, :].rearrange("p c d -> p (c d)"),
                             ctx_in[bass.ds(step.n - k, 1), :, :].rearrange("o (p c) d -> (o p) (c d)", c=KC)).then_inc(c_in[side], 16)

            def load_expert(e):
                if isinstance(e, int) and e == 0:
                    sp.wait_ge(s["bx_psum"], 1)
                    sp.wait_ge(s["m_psum"], 1)
                for q in (3, 0, 2, 1):
                    if not (isinstance(e, int) and e == 0):
                        sp.wait_ge(s[f"lo_ready{q}"], e)
                        sp.wait_ge(s[f"hi_ready{q}"], e)
                        waited(sp)
                    if q < 2:
                        src = w1[bass.ds(e, 1), q * P:(q + 1) * P, :].rearrange("o p f -> p (o f)")
                        sp.dma_start(stage[:, q * QW:(q + 1) * QW], src).then_inc(s[f"stage_in{q}"], 16)
                    else:
                        h = q - 2
                        src = w2[bass.ds(e, 1), h * F // 2:(h + 1) * F // 2, :].rearrange("o (c p) d -> p (o c) d", p=P)
                        sp.dma_start(stage[:, q * QW:(q + 1) * QW].rearrange("p (c d) -> p c d", d=D), src).then_inc(s[f"stage_in{q}"], 16)

            def load(name, dst, src):
                sp.dma_start(dst, src, allow_slow_non_contiguous=True).then_inc(s[name], 16)

            def load_weight(name, dst, src):
                load(name, dst, src.rearrange("(c p) e -> p c e", p=P))

            def step(p):
                if p.g is not None:
                    sp.wait_ge(s["x2_ready"], p.g + 1)
                    sp.dma_start(x2_rows[bass.ds(p.g * S, S), :], x2[:, :]).then_inc(s["x2_stored"], 16)
                if p.batch(1) is not None and not (isinstance(p.n, int) and p.n < 3):
                    load_ctx(1, p)
                if not (isinstance(p.n, int) and p.n in (FIRST - 1 + E, *range(FIRST - 1))):
                    load_expert(p.n - FIRST + 1)

            sp.sem_inc(s["x2_stored"], 16)
            load("x0_in", x_all[:, 0, :], x[0])
            load_weight("wqk_in", wqk_s[:, :, :], w_qk)
            load("slope_in", slope_c[:, :], slope.partition_broadcast(S))
            load("x_in", x_all[:, 1:B, :], x[1:B].rearrange("b s d -> s b d"))
            load_weight("wv_in", raw_wv, w_v)
            load_weight("a_in", raw_wq, wq)
            load_weight("a_in", raw_wk, wk)
            load("a_in", bq_col[:, :], bq.rearrange("(c p) -> p c", p=P))
            load_ctx(0, Step(0, 0))
            load_weight("m_in", raw_wo, wo)
            load_weight("m_in", raw_xv, w_xv)
            load("m_in", bv_col[:, :], bv.rearrange("(c p) -> p c", p=P))
            load("m_in", bo_row[:, :], bo.rearrange("(o d) -> o d", o=1))
            load_ctx(0, Step(0, 1))
            load("gate_in", gw_raw[:, :], gate_w)
            load("gate_in", gb_raw[:, 0, :], gate_b.partition_broadcast(S))
            load("gate_in", gb_raw[:, 1, :], expert_bias.partition_broadcast(S))
            load("b1_in", b1_raw[:, :], b1.rearrange("e (c p) -> (e c) p", p=P))
            load("b2_raw_in", b2_raw[:, :], b2)
            run_steps(sp, step)

        @block.gpsimd
        def _(pool):
            pool.memset(ident[:, :], 0.0).then_inc(s["ident_ready"], 1)
            pool.wait_ge(s["ident_ready"], 1)
            pool.affine_select(out=ident[:, :], in_=ident[:, :], compare_op=ALU.not_equal, fill=1.0, base=0,
                               pattern=[[-1, P]], channel_multiplier=1).then_inc(s["ident_ready"], 1)

            def rstd(n, k, rows):
                var = st[0:rows, 8 * n + 2:8 * n + 3]
                pool.wait_ge(s[f"y{n}_agg"], k + 1)
                pool.tensor_tensor(var, var, st[0:rows, 40:41], ALU.add).then_inc(s[f"y{n}_eps"], 1)
                pool.wait_ge(s[f"y{n}_eps"], k + 1)
                pool.tensor_tensor(var, var, st[0:rows, 41:42], ALU.pow).then_inc(s[f"y{n}_rstd"], 1)

            def split_lo(p, q):
                e = p.n - FIRST
                pool.wait_ge(s[f"hi_ready{q}"], e + 1)
                pool.wait_ge(s[f"stage_in{q}"], 16 * (e + 1))
                pool.tensor_tensor(part(w_lo, e, q), staged(q), part(w_hi, e, q), ALU.subtract).then_inc(s[f"lo_ready{q}"], 1)

            def add_bias(p):
                side, before = p.half(2)
                pool.wait_ge(s["x1_ready"], p.c + 1)
                if not (isinstance(before, int) and before == 0):
                    pool.wait_ge(s["y2_ready"], p.c - 1)
                pool.wait_ge(s["bx_ready"], 1)
                pool.tensor_tensor(x1b[side][:, :], x1[:, :], b_x[:, :], ALU.add).then_inc(s["x1b_ready"], 1)

            pool.iota(iota_i[:, 0:P], pattern=[[1, P]], base=0, channel_multiplier=-1).then_inc(s["ones_ready"], 1)
            pool.iota(iota_i[:, P:2 * P], pattern=[[1, P]], base=0, channel_multiplier=0).then_inc(s["ones_ready"], 1)
            pool.iota(iota_i[:, 2 * P:2 * P + B], pattern=[[S, B]], base=0, channel_multiplier=1).then_inc(s["ones_ready"], 1)
            pool.memset(st[:, 40:41], EPS).then_inc(s["ones_ready"], 1)
            pool.memset(st[:, 41:42], -0.5).then_inc(s["ones_ready"], 1)
            pool.memset(ones[:, :], 1.0).then_inc(s["ones_ready"], 1)
            pool.memset(ones3[:, :], 0.0).then_inc(s["ident_ready"], 1)
            pool.memset(ones16[:, :], 1.0).then_inc(s["ones_ready"], 1)
            pool.wait_ge(s["ident_ready"], 3)
            pool.memset(ones3[0:3, :], 1.0).then_inc(s["ones_ready"], 1)
            pool.wait_ge(s["ones_ready"], 8)
            pool.affine_select(out=low16[:, :], in_=ones16[:, :], compare_op=ALU.is_gt, fill=0.0, base=0,
                               pattern=[[1, P]], channel_multiplier=-1).then_inc(s["ones_ready"], 1)
            pool.wait_ge(s["alibi_flat"], 1)
            pool.affine_select(out=alibi[:, :], in_=alibi[:, :], compare_op=ALU.is_ge, fill=MASKED, base=0,
                               pattern=[[-1, S]], channel_multiplier=1).then_inc(s["alibi_ready"], 1)

            def copy_x(p):
                side, _ = p.half(0)
                if isinstance(p.a, int):
                    pool.wait_ge(s["x_in" if p.a else "x0_in"], 16)
                if not (isinstance(p.a, int) and p.a < 2):
                    pool.wait_ge(s["uT_psum"], p.a - 1)
                pool.tensor_tensor(xw[side][:, :], x_all[:, bass.ds(p.a, 1), :].rearrange("p o d -> p (o d)"),
                                   ones[0:S, 0:1].to_broadcast([S, D]), ALU.mult).then_inc(s["xw_ready"], 1)

            def step(p):
                if p.a is not None:
                    copy_x(p)
                if p.c is not None:
                    rstd(1, p.c, S)
                if p.g is not None:
                    rstd(2, p.g, S)
                if p.c is not None:
                    add_bias(p)
                if has_expert(p):
                    split_lo(p, 0)
                    split_lo(p, 1)

            def between(n):
                if n == 1:
                    pool.memset(b2_rows[:, :].bitcast(F32), 0.0).then_inc(s["b2_zeroed"], 1)
                if n == 3:
                    pool.wait_ge(s["b2_split"], 1)
                    pool.dma_start(b2_parts.rearrange("n e d -> e n d"), b2_split[:, :, :]).then_inc(s["b2_stored"], 16)

            run_steps(pool, step, between)
            pool.wait_ge(s["b2_stored"], 16)
            pool.wait_ge(s["b2_zeroed"], 1)
            pool.dma_start(b2_rows[0:3, :], b2_parts.rearrange("n e d -> n (e d)")).then_inc(s["b2_in"], 16)

            last_row = pool.to_reg(N - 1)

            def gather(u, k):
                pool.wait_ge(idx_ready[u], k + 1)
                waited(pool)
                pool.indirect_dma_start(xg[u], None, x2_rows, bass.IndirectOffsetOnAxis(ap=idx_in[u][:, :].bitcast(U32), axis=0),
                                        bounds_check=last_row, oob_is_err=False).then_inc(gathered[u], 16)

            def keep(u, k):
                pool.wait_ge(gathered[u], 16 * (k + 1))
                pool.wait_ge(s["y3_ready"], 2 * k + u + 1)
                waited(pool)
                pool.tensor_scalar(x_keep, xg[u], 1.0, 0.0, ALU.mult, ALU.add).then_inc(s["kept"], 1)
                pool.wait_ge(s["kept"], 2 * k + u + 1)
                pool.wait_ge(s["xgT_psum"], 2 * k + u + 1)

            pool.wait_ge(s["x2_stored"], 16 * (B + 1))
            gather(0, 0)
            gather(1, 0)
            pool.wait_ge(s["used_ready"], 2)
            used = pool.value_load(slots_used[0:1, 0:1], min_val=TILES, max_val=SLOTS)
            with pool.Fori(0, SLOTS // 2) as t:
                for u in range(2):
                    with pool.If(2 * t + u < used):
                        keep(u, t)
                        gather(u, t + 1)
                        rstd(3, 2 * t + u, P)
                        pool.wait_ge(s["o_ready"], 2 * t + u + 1)
                        pool.wait_ge(oidx_ready[u], t + 1)
                        waited(pool)
                        pool.indirect_dma_start(out.rearrange("b s d -> (b s) d"),
                                                bass.IndirectOffsetOnAxis(ap=idx_out[u][:, :].bitcast(U32), axis=0),
                                                y3n[u], None, bounds_check=last_row, oob_is_err=False).then_inc(scattered[u], 16)
            for u in range(2):
                slots = (used + 1 - u) // 2
                pool.wait_ge(scattered[u], 16 * slots)
                pool.wait_ge(gathered[u], 16 * (slots + 1))

        @block.scalar
        def _(act):
            def copy(dst, src, scale=1.0):
                return act.activation(dst, src, ACT.Copy, scale=scale)

            def split_hi(p, q):
                e = p.n - FIRST
                act.wait_ge(s[f"stage_in{q}"], 16 * (e + 1))
                copy(part(w_hi, e, q), staged(q)).then_inc(s[f"hi_ready{q}"], 1)

            def step(p):
                if p.b is not None:
                    act.wait_ge(s["pT_psum"], p.b + 1)
                    copy(pT[:, :], bank[1][0:S, 0:S]).then_inc(s["pT_ready"], 1)
                if p.d is not None:
                    act.wait_ge(s["pcT_psum"], p.d + 1)
                    copy(pcT[:, :, :], bank[2][0:SP_, 0:KC * S].rearrange("p (c n) -> p c n", c=KC)).then_inc(s["pcT_ready"], 1)
                if p.b is not None:
                    act.wait_ge(s["uT_psum"], p.b + 1)
                    copy(uT[:, :, :], cols2(4)).then_inc(s["uT_ready"], 1)
                if p.a is not None:
                    act.wait_ge(s["xT_psum"], p.a + 1)
                    copy(xT[:, :, :], cols2(0)).then_inc(s["xT_ready"], 1)
                if has_expert(p):
                    split_hi(p, 2)
                if p.d is not None:
                    act.wait_ge(s["ccT_psum"], p.d + 1)
                    copy(ccT[:, :, :], cols2(1)).then_inc(s["ccT_ready"], 1)
                if p.c is not None:
                    act.wait_ge(s["x1T_psum"], p.c + 1)
                    copy(x1T[:, :, :], cols2(3)).then_inc(s["x1T_ready"], 1)
                if p.a is not None:
                    act.wait_ge(s["gT_psum"], p.a + 1)
                    copy(gT[:, :, :], cols2(0), SCALE).then_inc(s["gT_ready"], 1)
                if p.g is not None:
                    act.wait_ge(s["x2T_psum"], p.g + 1)
                    copy(x2T[:, :, :], cols2(7)).then_inc(s["x2T_ready"], 1)
                if p.c is not None:
                    act.wait_ge(s["cT_psum"], p.c + 1)
                    copy(cT[:, 0, :], bank[5][:, 0:SK]).then_inc(s["cT_ready"], 1)
                    act.wait_ge(s["rT_psum"], p.c + 1)
                    act.wait_ge(s["c_ready"], 1)
                    for d in range(DC):
                        act.activation(rT[:, d, :], cols2(2)[:, d, :], ACT.Identity, bias=c_x[:, d:d + 1]).then_inc(s["rT_ready"], 1)
                if p.a is not None:
                    act.wait_ge(s["sc_max"], p.a + 1)
                    act.activation(pr[:, :], sc[:, :], ACT.Exp, bias=st[0:S, 0:1], accum_out=st[0:S, 1:2]).then_inc(s["p_ready"], 1)
                if has_expert(p):
                    split_hi(p, 1)
                if p.c is not None:
                    act.wait_ge(s["sc2_max"], p.c + 1)
                    act.activation(pc[:, :], bank[5][0:S, 0:SK], ACT.Exp, bias=st[0:S, 2:3], accum_out=st[0:S, 3:4]).then_inc(s["pc_ready"], 1)

            def between(n):
                if n == 1:
                    act.wait_ge(s["wvT_psum"], 1)
                    copy(wvT[:, :, :], bank[4][:, :].rearrange("p (c d) -> p c d", c=DC)).then_inc(s["wvT_ready"], 1)
                if n == 2:
                    act.wait_ge(s["a_psum"], 1)
                    copy(a_x[:, :, :], bank[6][:, :].rearrange("p (c d) -> p c d", c=DC), SCALE).then_inc(s["a_ready"], 1)
                    act.wait_ge(s["c_psum"], 1)
                    copy(c_x[:, :], bank[5][:, 0:DC], SCALE).then_inc(s["c_ready"], 1)
                    act.wait_ge(s["woT_psum"], 1)
                    copy(woT, bank[7][:, :].rearrange("p (c d) -> p c d", c=DC)).then_inc(s["woT_ready"], 1)
                if n == 3:
                    act.wait_ge(s["m_psum"], 1)
                    copy(m_x[:, :, :], bank[6][:, :].rearrange("p (c d) -> p c d", c=DC)).then_inc(s["m_ready"], 1)
                    act.wait_ge(s["gwT_psum"], 1)
                    copy(gwT[:, :, :], bank[2][:, 0:DC * E].rearrange("p (c d) -> p c d", c=DC)).then_inc(s["gwT_ready"], 1)
                    act.wait_ge(s["bx_psum"], 1)
                    copy(b_x[:, :], bank[7][0:S, 0:D]).then_inc(s["bx_ready"], 1)
                    copy(b1T[:, :], bank[2][:, DC * E:DC * E + E * FC]).then_inc(s["b1_ready"], 1)

            run_steps(act, step, between)

            def xg_evacuated(n):
                act.wait_ge(s["xgT_psum"], n + 1)
                copy(xgT_hi, cols2(6, P)).then_inc(s["xgT_hi_ready"], 1)

            xg_evacuated(0)
            act.wait_ge(s["b1_ready"], 1)
            act.wait_ge(s["used_ready"], 2)
            used = act.value_load(slots_used[0:1, 0:1], min_val=TILES, max_val=SLOTS)
            with act.Fori(0, SLOTS // 2) as t:
                for u in range(2):
                    n = 2 * t + u
                    with act.If(n < used):
                        e = act.value_load(slot_expert[0:1, bass.ds(n, 1)], min_val=0, max_val=E - 1)
                        for q in range(4):
                            act.wait_ge(s[f"h{q}_psum"], n + 1)
                            for k in range(FC // 4):
                                c = q * FC // 4 + k
                                last = act.activation(hid[:, c * P:(c + 1) * P], bank[q][:, k * P:(k + 1) * P], ACT.Relu,
                                                      bias=b1T[:, bass.ds(e * FC + c, 1)])
                            last.then_inc(s[f"h{q}_ready"], 1)
                        xg_evacuated(n + 1)

        @block.vector
        def _(dve):
            done = [0]

            def link(ins):
                done[0] += 1
                ins.then_inc(s["route"], 1)
                dve.wait_ge(s["route"], done[0])

            dve.wait_ge(s["ones_ready"], 9)
            dve.wait_ge(s["slope_in"], 16)
            dve.tensor_copy(num[:, :], iota_i[0:S, P:2 * P])
            dve.tensor_copy(num16[:, :], iota_i[0:S, P:2 * P])
            link(dve.tensor_copy(sc[:, :], iota_i[0:S, 0:S]))
            dve.tensor_scalar(alibi[:, :], sc[:, :], slope_c[:, 0:1], None, ALU.mult).then_inc(s["alibi_flat"], 1)

            def ln_mean(n, y, rows, k):
                part = st[0:rows, 38 + 6 * n:44 + 6 * n]
                dve.wait_ge(s[f"y{n}_ready"], k + 1 + (n == 3))
                dve.bn_stats(part, y).then_inc(s[f"y{n}_bn"], 1)

            def ln_merge(n, rows, k):
                part = st[0:rows, 38 + 6 * n:44 + 6 * n]
                dve.wait_ge(s[f"y{n}_bn"], k + 1)
                waited(dve)
                dve.bn_aggr(st[0:rows, 8 * n + 1:8 * n + 3], part).then_inc(s[f"y{n}_agg"], 1)

            def ln_apply(n, dst, y, rows, k):
                dve.wait_ge(s[f"y{n}_rstd"], k + 1)
                return dve.tensor_scalar(dst, y, st[0:rows, 8 * n + 1:8 * n + 2], st[0:rows, 8 * n + 2:8 * n + 3],
                                         ALU.subtract, ALU.mult)

            def split_hi(p, q):
                e = p.n - FIRST
                dve.wait_ge(s[f"stage_in{q}"], 16 * (e + 1))
                dve.tensor_copy(part(w_hi, e, q), staged(q)).then_inc(s[f"hi_ready{q}"], 1)

            def split_lo(p, q):
                e = p.n - FIRST
                dve.wait_ge(s[f"hi_ready{q}"], e + 1)
                dve.wait_ge(s[f"stage_in{q}"], 16 * (e + 1))
                dve.tensor_tensor(part(w_lo, e, q), staged(q), part(w_hi, e, q), ALU.subtract).then_inc(s[f"lo_ready{q}"], 1)

            def step(p):
                if p.b is not None:
                    dve.wait_ge(s["p_ready"], p.b + 1)
                    dve.reciprocal(st[0:S, 4:5], st[0:S, 1:2]).then_inc(s["p_inv"], 1)
                if p.d is not None:
                    dve.wait_ge(s["pc_ready"], p.d + 1)
                    dve.reciprocal(st[0:S, 5:6], st[0:S, 3:4]).then_inc(s["pc_inv"], 1)
                if p.c is not None:
                    if not (isinstance(p.c, int) and p.c == 0):
                        dve.wait_ge(s["x1b_ready"], p.c)
                    ln_apply(1, x1[:, :], y1[:, :], S, p.c).then_inc(s["x1_ready"], 1)
                if p.g is not None:
                    dve.wait_ge(s["x2_stored"], 16 * p.g + 16)
                    ln_apply(2, x2[:, :], y2[:, :], S, p.g).then_inc(s["x2_ready"], 1)
                if has_expert(p):
                    split_hi(p, 0)
                    split_hi(p, 3)
                    split_lo(p, 3)
                if p.c is not None:
                    dve.wait_ge(s["cT_psum"], p.c + 1)
                    dve.tensor_copy(cT[:, 1, :], bank[6][:, 0:SK]).then_inc(s["cT_ready"], 1)
                if p.a is not None:
                    dve.wait_ge(s["sc_psum"], p.a + 1)
                    dve.wait_ge(s["alibi_ready"], 1)
                    dve.tensor_tensor(sc[:, :], bank[3][0:S, 0:S], alibi[:, :], ALU.add).then_inc(s["sc_biased"], 1)
                    dve.wait_ge(s["sc_biased"], p.a + 1)
                    dve.tensor_reduce(st[0:S, 0:1], sc[:, :], AX.X, ALU.max, negate=True).then_inc(s["sc_max"], 1)
                if has_expert(p):
                    split_lo(p, 2)
                if p.g is not None:
                    dve.wait_ge(s["gate_psum"], p.g + 1)
                    dve.wait_ge(s["logit_ready"], 1)
                    dve.tensor_tensor(logit[:, bass.ds(p.g, 1), :].rearrange("p o e -> p (o e)"), bank[7][0:S, 0:E],
                                      gb[:, :], ALU.add).then_inc(s["logit_ready"], 1)
                if p.c is not None:
                    dve.wait_ge(s["sc2_psum"], p.c + 1)
                    dve.tensor_reduce(st[0:S, 2:3], bank[5][0:S, 0:SK], AX.X, ALU.max, negate=True).then_inc(s["sc2_max"], 1)
                if p.b is not None:
                    dve.wait_ge(s["out1_psum"], p.b + 1)
                    dve.wait_ge(s["p_inv"], p.b + 1)
                    dve.wait_ge(s["x0_in"], 16)
                    dve.wait_ge(s["x_in"], 16)
                    dve.scalar_tensor_tensor(y1[:, :], bank[4][0:S, 0:D], st[0:S, 4:5],
                                             x_all[:, bass.ds(p.b, 1), :].rearrange("p o d -> p (o d)"),
                                             ALU.mult, ALU.add).then_inc(s["y1_ready"], 1)
                    ln_mean(1, y1[:, :], S, p.b)
                if p.d is not None:
                    dve.wait_ge(s["out2_psum"], p.d + 1)
                    dve.wait_ge(s["pc_inv"], p.d + 1)
                    dve.wait_ge(s["x1b_ready"], p.d + 1)
                    dve.scalar_tensor_tensor(y2[:, :], bank[6][0:S, 0:D], st[0:S, 5:6], x1b[p.half(3)[0]][:, :],
                                             ALU.mult, ALU.add).then_inc(s["y2_ready"], 1)
                if p.b is not None:
                    ln_merge(1, S, p.b)
                if p.d is not None:
                    ln_mean(2, y2[:, :], S, p.d)
                if p.d is not None:
                    ln_merge(2, S, p.d)

            def between(n):
                if n == 1:
                    dve.wait_ge(s["m_in"], 16 * 4)
                    dve.tensor_copy(bv_wide[:, :, :], bv_col[:, :].unsqueeze(2).to_broadcast([P, DC, S])).then_inc(s["wide_ready"], 1)
                    dve.wait_ge(s["gate_in"], 16 * 3)
                    dve.tensor_tensor(gb[:, :], gb_raw[:, 0, :], gb_raw[:, 1, :], ALU.add).then_inc(s["logit_ready"], 1)
                if n != 2:
                    return
                dve.wait_ge(s["b2_raw_in"], 16)
                hi, mid, low = (b2_split[:, n, :] for n in range(3))
                link(dve.tensor_copy(hi, b2_raw[:, :]))
                link(dve.tensor_tensor(b2_raw[:, :], b2_raw[:, :], hi, ALU.subtract))
                link(dve.tensor_copy(mid, b2_raw[:, :]))
                link(dve.tensor_tensor(b2_raw[:, :], b2_raw[:, :], mid, ALU.subtract))
                dve.tensor_copy(low, b2_raw[:, :]).then_inc(s["b2_split"], 1)

            run_steps(dve, step, between)

            scratch = Room()
            scratch.at = 4800

            def room(*shape):
                return scratch.take(S, *shape)

            order = [0]

            def do(ins, *after):
                order[0] += 1
                ins.then_inc(s["route2"], 1)
                return order[0]

            def need(n):
                dve.wait_ge(s["route2"], n)

            def rows(v, n):
                return v.unsqueeze(1).to_broadcast([S, n, v.shape[-1]])

            def cols(v, n):
                return v.unsqueeze(2).to_broadcast([S, v.shape[-1], n])

            token = room(B)
            back = room(E)
            bound = room(TILES)
            earlier = room(E, E)
            dve.tensor_copy(token, iota_i[0:S, 2 * P:2 * P + B])
            dve.tensor_scalar(back, num[:, 0:E], -1.0, float(E), ALU.mult, ALU.add)
            dve.tensor_scalar(bound, num[:, 0:TILES], float(P), None, ALU.mult)
            need(do(dve.tensor_tensor(earlier, rows(num[:, 0:E], E), cols(num[:, 0:E], E), ALU.is_lt)))

            top = room(B)
            hot = room(B, E)
            pick = room(B)
            dve.wait_ge(s["logit_ready"], B + 1)
            need(do(dve.tensor_reduce(top, logit[:, :, :], AX.X, ALU.max)))
            need(do(dve.tensor_tensor(hot, logit[:, :, :], cols(top, E), ALU.is_equal)))
            need(do(dve.tensor_tensor(hot, hot, rows(back, B), ALU.mult)))
            need(do(dve.tensor_reduce(pick, hot, AX.X, ALU.max)))
            dve.tensor_tensor(oh16[:, :, :], cols(pick, E), rows(back, B), ALU.is_equal).then_inc(s["hot_ready"], 1)
            is_hot = do(dve.tensor_tensor(hot, cols(pick, E), rows(back, B), ALU.is_equal))

            more = room(E, TILES)
            tiles = room(E)
            before = room(E, E)
            first = room(E)
            rank = room(B, E)
            mine = room(B)
            over = room(B, TILES - 1)
            tile = room(B)
            place = room(B)
            base = room(B)
            slot = room(B)
            dve.wait_ge(s["rank_psum"], 1)
            a = do(dve.tensor_tensor(more, cols(bank[1][0:S, 0:E], TILES), rows(bound, E), ALU.is_gt))
            need(is_hot)
            b = do(dve.tensor_tensor(rank, hot, bank[0][0:S, 0:B * E].rearrange("p (b e) -> p b e", e=E), ALU.mult))
            need(a)
            a = do(dve.tensor_reduce(tiles, more, AX.X, ALU.add))
            need(b)
            b = do(dve.tensor_reduce(mine, rank, AX.X, ALU.add))
            need(a)
            a = do(dve.tensor_tensor(before, earlier, rows(tiles, E), ALU.mult))
            need(b)
            b = do(dve.tensor_tensor(over, cols(mine, TILES - 1), rows(bound[:, 1:TILES], B), ALU.is_ge))
            need(a)
            a = do(dve.tensor_reduce(first, before, AX.X, ALU.add))
            need(b)
            b = do(dve.tensor_reduce(tile, over, AX.X, ALU.add))
            need(a)
            a = do(dve.tensor_tensor(rank, hot, rows(first, B), ALU.mult))
            need(b)
            b = do(dve.scalar_tensor_tensor(place, tile, -float(P), mine, ALU.mult, ALU.add))
            need(a)
            a = do(dve.tensor_reduce(base, rank, AX.X, ALU.add))
            need(b)
            for k in range(B // 2):
                dve.tensor_scalar(place16[:, k, :], num16[:, :], place[:, k:k + 1], None, ALU.is_equal)
            need(a)
            a = do(dve.tensor_tensor(slot, base, tile, ALU.add))
            for k in range(B // 2, B):
                dve.tensor_scalar(place16[:, k, :], num16[:, :], place[:, k:k + 1], None, ALU.is_equal)
            need(a)
            need(do(dve.tensor_tensor(slot16[:, :, 1, :], rows(num[:, 0:COLS], B), cols(slot, COLS), ALU.is_equal)))
            dve.tensor_tensor(slot16[:, :, 0, :], slot16[:, :, 1, :], cols(token, COLS), ALU.mult).then_inc(s["table16_ready"], 1)
            starts = room(COLS, E - 1)
            owner = room(COLS)
            total = room(1)
            a = do(dve.tensor_tensor(starts, cols(num[:, 0:COLS], E - 1), rows(first[:, 1:E], COLS), ALU.is_ge))
            b = do(dve.tensor_reduce(total, tiles, AX.X, ALU.add))
            need(a)
            a = do(dve.tensor_reduce(owner, starts, AX.X, ALU.add))
            need(b)
            dve.tensor_copy(slots_used[:, 0:1], total[0:1, :]).then_inc(s["used_ready"], 1)
            need(a)
            dve.tensor_copy(slot_expert[:, :], owner[0:1, :]).then_inc(s["used_ready"], 1)

            dve.wait_ge(s["table_psum"], 1)
            for u in range(2):
                dve.tensor_copy(idx_in[u][:, :], bank[5][:, u:u + 1]).then_inc(idx_ready[u], 1)
            unused = y3[:, 0:COLS]
            need(do(dve.tensor_scalar(unused, bank[5][:, COLS:2 * COLS], -float(DROP), float(DROP), ALU.mult, ALU.add)))
            do(dve.tensor_copy(row_in[:, :], bank[5][:, 0:COLS]))
            need(do(dve.tensor_tensor(row_out[:, :], bank[5][:, 0:COLS], unused, ALU.add)))

            dve.sem_inc(s["y3_ready"], 1)

            def flat(v):
                return v.rearrange("p c n -> p (c n)")

            def xg_rest(n):
                dve.wait_ge(s["xgT_hi_ready"], n + 1)
                dve.tensor_tensor(xgT_lo, cols2(6, P), xgT_hi, ALU.subtract).then_inc(s["xgT_lo_ready"], 1)

            def y3n_apply(dst, k):
                ln_apply(3, dst, y3, P, k).then_inc(s["o_ready"], 1)

            def slot(t, u):
                n = 2 * t + u
                for q in range(4):
                    at = slice(q * QF, (q + 1) * QF)
                    dve.wait_ge(s[f"h{q}_ready"], n + 1)
                    dve.tensor_copy(flat(hid_hi)[:, at], hid[:, at]).then_inc(s[f"hi{q}_ready"], 1)
                    dve.wait_ge(s[f"hi{q}_ready"], n + 1)
                    dve.tensor_tensor(flat(hid_lo)[:, at], hid[:, at], flat(hid_hi)[:, at], ALU.subtract).then_inc(s[f"lo{q}_ready"], 1)
                    if q == 1 and not (isinstance(n, int) and n == 0):
                        y3n_apply(y3n[1 - u], n - 1)
                dve.tensor_copy(idx_in[u][:, :], row_in[:, bass.ds(n + 2, 1)]).then_inc(idx_ready[u], 1)
                if not (isinstance(t, int) and t == 0):
                    dve.wait_ge(scattered[u], 16 * t)
                dve.tensor_copy(idx_out[u][:, :], row_out[:, bass.ds(n, 1)]).then_inc(oidx_ready[u], 1)
                xg_rest(n + 1)
                dve.wait_ge(s["kept"], n + 1)
                dve.wait_ge(s["y3_psum"], n + 1)
                dve.tensor_tensor(y3, bank[4][:, 0:D], x_keep, ALU.add).then_inc(s["y3_ready"], 1)
                ln_mean(3, y3, P, n)
                ln_merge(3, P, n)

            xg_rest(0)
            dve.wait_ge(s["used_ready"], 2)
            used = dve.value_load(slots_used[0:1, 0:1], min_val=TILES, max_val=SLOTS)
            for u in range(2):
                slot(0, u)
            with dve.Fori(1, SLOTS // 2) as t:
                for u in range(2):
                    with dve.If(2 * t + u < used):
                        slot(t, u)
            y3n_apply(y3n_both[:, bass.ds((used + 1) % 2 * D, D)], used - 1)

        @block.tensor
        def _(pe):
            def mm(dst, lhsT, rhs, k, last):
                return pe.matmul(dst, lhsT, rhs, start=(k == 0), stop=(k == last))

            def project(dst, weights, act_T):
                for e in range(DC):
                    for d in range(DC):
                        last = mm(dst[:, e, :], weights[:, d, e * P:(e + 1) * P], act_T[:, d, :], d, DC - 1)
                return last

            def flip(b, src, rows):
                for d in range(DC):
                    last = pe.transpose(cols2(b, rows)[:, d, :], src[:, d * P:(d + 1) * P], ident[0:rows, 0:rows])
                return last

            def flip_weights(b, src):
                dst = bank[b][:, :].rearrange("p (c d) -> p c d", c=DC)
                for d in range(DC):
                    for e in range(DC):
                        last = pe.transpose(dst[:, d, e * P:(e + 1) * P], src[:, e, d * P:(d + 1) * P], ident[:, :])
                return last

            def step(p):
                if p.b is not None:
                    pe.wait_ge(s["p_ready"], p.b + 1)
                    pe.transpose(bank[1][0:S, 0:S], pr[:, :], ident[0:S, 0:S]).then_inc(s["pT_psum"], 1)
                if p.d is not None:
                    pe.wait_ge(s["pc_ready"], p.d + 1)
                    for k in range(KC):
                        last = pe.transpose(bank[2][0:SP_, k * S:(k + 1) * S], pc[:, k * SP_:(k + 1) * SP_], ident[0:S, 0:S])
                    last.then_inc(s["pcT_psum"], 1)
                if p.b is not None:
                    pe.wait_ge(s["pT_ready"], p.b + 1)
                    if not (isinstance(p.b, int) and p.b == 0):
                        pe.wait_ge(s["y1_ready"], p.b)
                    for d in range(DC):
                        last = mm(cols2(4)[:, d, :], xw[p.half(1)[0]][:, d * P:(d + 1) * P], pT[:, :], 0, 0)
                    last.then_inc(s["uT_psum"], 1)
                if p.a is not None:
                    pe.wait_ge(s["xw_ready"], p.a + 1)
                    flip(0, xw[p.half(0)[0]], S).then_inc(s["xT_psum"], 1)
                if p.d is not None:
                    side, _ = p.half(3)
                    pe.wait_ge(s["pcT_ready"], p.d + 1)
                    for d in range(DC):
                        for k in range(KC):
                            last = mm(cols2(1)[:, d, :], cw[side][:, k, d * P:(d + 1) * P], pcT[:, k, :], k, KC - 1)
                    last.then_inc(s["ccT_psum"], 1)
                if p.c is not None:
                    pe.wait_ge(s["x1_ready"], p.c + 1)
                    pe.wait_ge(s["sc_biased"], p.c + 2 if p.batch(1) is not None else B)
                    flip(3, x1, S).then_inc(s["x1T_psum"], 1)
                if p.a is not None:
                    pe.wait_ge(s["xT_ready"], p.a + 1)
                    pe.wait_ge(s["wqk_in"], 16)
                    project(cols2(0), wqk_s, xT).then_inc(s["gT_psum"], 1)
                if p.g is not None:
                    pe.wait_ge(s["x2_ready"], p.g + 1)
                    pe.wait_ge(s["logit_ready"], p.g + 1)
                    flip(7, x2, S).then_inc(s["x2T_psum"], 1)
                if p.c is not None:
                    side, before = p.half(2)
                    pe.wait_ge(c_in[side], 16 * (before + 1))
                    if not (isinstance(p.d, int) or p.d is None) or (isinstance(p.d, int) and p.d > 0):
                        pe.wait_ge(s["y2_ready"], p.d)
                    for d in range(DC):
                        for k in range(KC):
                            last = pe.transpose(bank[5 + d][:, k * SP_:(k + 1) * SP_], cw[side][:, k, d * P:(d + 1) * P], ident[0:SP_, 0:SP_])
                    last.then_inc(s["cT_psum"], 1)
                    pe.wait_ge(s["x1T_ready"], p.c + 1)
                    project(cols2(2), a_x, x1T).then_inc(s["rT_psum"], 1)
                if p.a is not None:
                    pe.wait_ge(s["gT_ready"], p.a + 1)
                    for d in range(DC):
                        last = mm(bank[3][0:S, 0:S], gT[:, d, :], xT[:, d, :], d, DC - 1)
                    last.then_inc(s["sc_psum"], 1)
                if p.g is not None:
                    pe.wait_ge(s["x2T_ready"], p.g + 1)
                    for d in range(DC):
                        last = mm(bank[7][0:S, 0:E], x2T[:, d, :], gwT[:, d, :], d, DC - 1)
                    last.then_inc(s["gate_psum"], 1)
                if p.c is not None:
                    pe.wait_ge(s["rT_ready"], DC * (p.c + 1))
                    pe.wait_ge(s["cT_ready"], DC * (p.c + 1))
                    for d in range(DC):
                        last = mm(bank[5][0:S, 0:SK], rT[:, d, :], cT[:, d, :], d, DC - 1)
                    last.then_inc(s["sc2_psum"], 1)
                if p.b is not None:
                    pe.wait_ge(s["uT_ready"], p.b + 1)
                    for d in range(DC):
                        last = mm(bank[4][0:S, 0:D], uT[:, d, :], wvT[:, d, :], d, DC - 1)
                    last.then_inc(s["out1_psum"], 1)
                if p.d is not None:
                    pe.wait_ge(s["ccT_ready"], p.d + 1)
                    for d in range(DC):
                        last = mm(bank[6][0:S, 0:D], ccT[:, d, :], m_x[:, d, :], d, DC - 1)
                    last.then_inc(s["out2_psum"], 1)

            def between(n):
                if n == 1:
                    pe.wait_ge(s["wv_in"], 16)
                    flip_weights(4, raw_wv).then_inc(s["wvT_psum"], 1)
                    pe.wait_ge(s["wvT_ready"], 1)
                if n == 2:
                    pe.wait_ge(s["a_in"], 16 * 3)
                    for d in range(DC):
                        for e in range(DC):
                            last = mm(bank[6][:, d * D:(d + 1) * D], raw_wq[:, e, d * P:(d + 1) * P], raw_wk[:, e, :], e, DC - 1)
                    last.then_inc(s["a_psum"], 1)
                    for d in range(DC):
                        for e in range(DC):
                            last = mm(bank[5][:, d:d + 1], raw_wk[:, e, d * P:(d + 1) * P], bq_col[:, e:e + 1], e, DC - 1)
                    last.then_inc(s["c_psum"], 1)
                    pe.wait_ge(s["m_in"], 16 * 4)
                    flip_weights(7, raw_wo).then_inc(s["woT_psum"], 1)
                    pe.wait_ge(s["a_ready"], 1)
                    pe.wait_ge(s["c_ready"], 1)
                if n == 3:
                    pe.wait_ge(s["woT_ready"], 1)
                    for d in range(DC):
                        for e in range(DC):
                            last = mm(bank[6][:, d * D:(d + 1) * D], raw_xv[:, e, d * P:(d + 1) * P], woT[:, e, :], e, DC - 1)
                    last.then_inc(s["m_psum"], 1)
                    pe.wait_ge(s["gate_in"], 16 * 3)
                    for d in range(DC):
                        last = pe.transpose(bank[2][:, d * E:(d + 1) * E], gw_raw[:, d * P:(d + 1) * P], ident[0:E, 0:E])
                    pe.wait_ge(s["b1_in"], 16)
                    pe.transpose(bank[2][:, DC * E:DC * E + E * FC], b1_raw[:, :], ident[0:E * FC, 0:E * FC]).then_inc(s["gwT_psum"], 1)
                    pe.wait_ge(s["wide_ready"], 1)
                    pe.wait_ge(s["ones_ready"], 9)
                    for e in range(DC):
                        mm(bank[7][0:S, 0:D], bv_wide[:, e, :], woT[:, e, :], e, DC)
                    mm(bank[7][0:S, 0:D], ones[0:1, 0:S], bo_row[:, :], DC, DC).then_inc(s["bx_psum"], 1)
                    for name in ("m_ready", "gwT_ready", "bx_ready", "b1_ready"):
                        pe.wait_ge(s[name], 1)

            pe.wait_ge(s["ident_ready"], 3)
            run_steps(pe, step, between)

            pe.wait_ge(s["hot_ready"], 1)
            for b in range(B - 1):
                pe.matmul(bank[0][:, (b + 1) * E:B * E], ones16[:, :],
                          oh16[:, b:b + 1, :].to_broadcast([S, B - 1 - b, E]), start=(b == 0), stop=False, skip_group_check=True)
            pe.matmul(bank[0][:, 0:B * E], low16[:, :], oh16[:, :, :].rearrange("p b e -> p (b e)"),
                      start=False, stop=True, skip_group_check=True)
            for b in range(B):
                last = mm(bank[1][:, 0:E], ones16[:, :], oh16[:, b, :], b, B - 1)
            last.then_inc(s["rank_psum"], 1)
            pe.wait_ge(s["table16_ready"], 1)
            for b in range(B):
                last = mm(bank[5][:, 0:2 * COLS], place16[:, b, :], slot16[:, b, :, :].rearrange("p t c -> p (t c)"), b, B - 1)
            last.then_inc(s["table_psum"], 1)

            def flip_rows(u, k):
                pe.wait_ge(gathered[u], 16 * (k + 1))
                flip(6, xg[u], P).then_inc(s["xgT_psum"], 1)

            flip_rows(0, 0)
            pe.wait_ge(s["used_ready"], 2)
            pe.wait_ge(s["b2_in"], 16)
            for q in range(4):
                pe.wait_ge(s[f"hi_ready{q}"], E)
                pe.wait_ge(s[f"lo_ready{q}"], E)
            used = pe.value_load(slots_used[0:1, 0:1], min_val=TILES, max_val=SLOTS)

            def slot(t, u):
                n = 2 * t + u
                e = pe.value_load(slot_expert[0:1, bass.ds(n, 1)], min_val=0, max_val=E - 1)
                pe.wait_ge(s["xgT_hi_ready"], n + 1)
                pe.wait_ge(s["xgT_lo_ready"], n + 1)
                for q in range(4):
                    for k in range(FC // 4):
                        c = q * FC // 4 + k
                        for d in range(DC):
                            at = bass.ds(e * WE + d * F + c * P, P)
                            dst = bank[q][:, k * P:(k + 1) * P]
                            pe.matmul(dst, w_hi[:, at], xgT_hi[:, d, :], start=(d == 0), stop=False)
                            pe.matmul(dst, w_hi[:, at], xgT_lo[:, d, :], start=False, stop=False)
                            last = pe.matmul(dst, w_lo[:, at], xgT_hi[:, d, :], start=False, stop=(d == DC - 1))
                    last.then_inc(s[f"h{q}_psum"], 1)
                flip_rows(1 - u, t + u)
                pe.wait_ge(s["y3_ready"], n + 1)
                for c in range(FC):
                    if c % (FC // 4) == 0:
                        pe.wait_ge(s[f"hi{c * 4 // FC}_ready"], n + 1)
                        pe.wait_ge(s[f"lo{c * 4 // FC}_ready"], n + 1)
                    at = bass.ds(e * WE + DC * F + c * D, D)
                    pe.matmul(bank[4][:, 0:D], hid_hi[:, c, :], w_hi[:, at], start=(c == 0), stop=False)
                    pe.matmul(bank[4][:, 0:D], hid_lo[:, c, :], w_hi[:, at], start=False, stop=False)
                    pe.matmul(bank[4][:, 0:D], hid_hi[:, c, :], w_lo[:, at], start=False, stop=False)
                pe.matmul(bank[4][:, 0:D], ones3[:, :], b2_rows[:, bass.ds(e * D, D)], start=False, stop=True).then_inc(s["y3_psum"], 1)

            with pe.Fori(0, SLOTS // 2) as t:
                for u in range(2):
                    with pe.If(2 * t + u < used):
                        slot(t, u)


_INS = ["x", "ctx_1024", "L0_attn_W_qk", "L0_attn_W_v", "L0_attn_alibi_slope", "L0_xattn_Wk", "L0_xattn_Wv",
        "L0_xattn_bv", "L0_xattn_Wq", "L0_xattn_bq", "L0_xattn_Wo", "L0_xattn_bo", "L0_ffn_gate_w", "L0_ffn_gate_b",
        "L0_ffn_expert_bias", "L0_ffn_w1", "L0_ffn_b1", "L0_ffn_w2", "L0_ffn_b2"]


def kernel(**inputs):
    import numpy as np
    import concourse.bacc as bacc
    from concourse.bass_utils import run_bass_kernel_spmd

    nc = bacc.Bacc("TRN2", target_bir_lowering=False, num_devices=1)
    arrays, args = {}, []
    for name in _INS:
        a = np.ascontiguousarray(inputs[name])
        arrays[f"in_{name}"] = a
        args.append(nc.dram_tensor(f"in_{name}", a.shape, mybir.dt.from_np(a.dtype), kind="ExternalInput").ap())
    out = nc.dram_tensor("out_0", inputs["x"].shape, F32, kind="ExternalOutput").ap()
    decoder_layer(nc, *args, out)
    r = run_bass_kernel_spmd(nc, [arrays], core_ids=[0])
    return r.results[0]["out_0"]
```

```python
from contextlib import ExitStack

import concourse.bass as bass
from concourse import mybir

F32 = mybir.dt.float32
BF16 = mybir.dt.bfloat16
F16 = mybir.dt.float16
I32 = mybir.dt.int32
U32 = mybir.dt.uint32
ALU = mybir.AluOpType
ACT = mybir.ActivationFunctionType
AX = mybir.AxisListType

P = 128
MASKED = -1.0e30
EPS = 1e-5
DROP = 4096


def decoder_layer(nc, x, ctx_in, w_qk, w_v, slope, wk, w_xv, bv, wq, bq, wo, bo,
                  gate_w, gate_b, expert_bias, w1, b1, w2, b2, out):
    B, S, D = x.shape
    SK = ctx_in.shape[1]
    E, _, F = w1.shape
    DC = D // P
    KC = 3
    SP_ = SK // KC
    FC = F // P
    N = B * S
    TILES = -(-N // P)
    SLOTS = TILES + E - 1
    COLS = SLOTS + 4
    WE = 2 * DC * F
    QW = WE // 4
    QF = F // 4
    FH = F // 2
    WARM = 20
    SCALE = float(D) ** -0.5
    assert S <= P and SP_ * KC == SK and SP_ <= P and DC == 2 and FC * D == DC * F

    with ExitStack() as stack:
        def sb(name, shape, dt=F32):
            return stack.enter_context(nc.sbuf_tensor(name, shape, dt))

        def sem(name):
            return stack.enter_context(nc.semaphore(name))

        x2_rows = nc.dram_tensor("x2_rows", [N, D], F32, kind="Internal").ap()
        b2_parts = nc.dram_tensor("b2_parts", [3, E, D], BF16, kind="Internal").ap()

        w_hi = sb("w_hi", [P, E * WE], F16)
        w_lo = sb("w_lo", [P, E * WE], BF16)
        b2_rows = sb("b2_rows", [P, E * D], BF16)
        b1T = sb("b1T", [P, E * FC])
        ident = sb("ident", [P, P])
        ones = sb("ones", [P, P])
        ones3 = sb("ones3", [P, P], BF16)
        alibi = sb("alibi", [S, S])
        num = sb("num", [S, P])
        num16 = sb("num16", [S, P], F16)
        iota_i = sb("iota_i", [P, 2 * P + B], I32)
        wqk_s = sb("wqk_s", [P, DC, D])
        wvT = sb("wvT", [P, DC, D])
        a_x = sb("a_x", [P, DC, D])
        m_x = sb("m_x", [P, DC, D])
        c_x = sb("c_x", [P, DC])
        b_x = sb("b_x", [S, D])
        gwT = sb("gwT", [P, DC, E])
        gb = sb("gb", [S, E])
        stage = sb("stage", [P, WE])
        raw = stage[:, 0:5 * DC * D].rearrange("p (n c d) -> p n c d", n=5, c=DC)
        raw_wv, raw_wo, raw_wq, raw_wk, raw_xv = (raw[:, n] for n in range(5))
        woT = raw_wq
        b1_raw = sb("b1_raw", [E * FC, P])
        b2_raw = sb("b2_raw", [E, D])
        b2_split = sb("b2_split", [E, 3, D], BF16)
        gw_raw = sb("gw_raw", [E, D])
        gb_raw = sb("gb_raw", [S, 2, E])
        bq_col = sb("bq_col", [P, DC])
        bv_col = sb("bv_col", [P, DC])
        bv_wide = sb("bv_wide", [P, DC, S])
        bo_row = sb("bo_row", [1, D])
        slope_c = sb("slope_c", [S, 1])
        xw = [sb(f"xw{u}", [S, D]) for u in range(2)]
        sc = sb("sc", [S, S])
        pr = sb("pr", [S, S])
        pT = sb("pT", [S, S])
        y1 = sb("y1", [S, D])
        x1 = sb("x1", [S, D])
        x1b = [sb(f"x1b{u}", [S, D]) for u in range(2)]
        x2 = sb("x2", [S, D])
        x2T = sb("x2T", [P, DC, S])
        work = sb("work", [P, 6400])

        class Room:

            def __init__(self):
                self.at = 0

            def take(self, rows, *shape, dt=F32):
                n = 1
                for d in shape:
                    n *= d
                words = n if dt == F32 else n // 2
                v = work[0:rows, self.at:self.at + words]
                self.at += words
                assert self.at <= work.shape[1]
                if dt != F32:
                    v = v.bitcast(dt)
                if len(shape) == 2:
                    v = v.rearrange("p (a b) -> p a b", b=shape[1])
                if len(shape) == 3:
                    v = v.rearrange("p (a b c) -> p a b c", b=shape[1], c=shape[2])
                return v

        own = sb("cw_own", [SP_, KC, D])
        room = Room()
        cw = [own[:, :, :], room.take(SP_, KC, D)]
        x_all = room.take(S, B, D)
        xT = room.take(P, DC, S)
        gT = room.take(P, DC, S)
        uT = room.take(P, DC, S)
        x1T = room.take(P, DC, S)
        rT = room.take(P, DC, S)
        cT = room.take(P, DC, SK)
        pc = room.take(S, SK)
        pcT = room.take(SP_, KC, S)
        ccT = room.take(P, DC, S)
        y2 = room.take(S, D)
        st = sb("st", [P, 64])
        logit = sb("logit", [S, B, E])
        oh16 = sb("oh16", [S, B, E], BF16)
        low16 = sb("low16", [S, P], BF16)
        ones16 = sb("ones16", [S, P], BF16)
        route_consts = sb("route_consts", [S, B + E + TILES + E * E])
        row_in = sb("row_in", [P, COLS], I32)
        row_out = sb("row_out", [P, COLS], I32)
        slot_expert = sb("slot_expert", [1, COLS], I32)
        pair_experts = sb("pair_experts", [1, COLS // 2], I32)
        slots_used = sb("slots_used", [1, 2], I32)
        idx_in = [sb(f"idx_in{u}", [P, 1], I32) for u in range(2)]
        idx_out = [sb(f"idx_out{u}", [P, 1], I32) for u in range(2)]

        room = Room()
        pre = room.take(P, F)
        hid = room.take(P, F)
        hid_hi = [room.take(P, F, dt=F16) for u in range(2)]
        hid_lo = [room.take(P, F, dt=BF16) for u in range(2)]
        routing_end = room.at
        xg = [room.take(P, D) for u in range(2)]
        xgT_hi = [room.take(P, DC, P, dt=F16) for u in range(2)]
        xgT_lo = [room.take(P, DC, P, dt=BF16) for u in range(2)]
        y3 = room.take(P, D)
        y3n = [room.take(P, D) for u in range(2)]
        x_keep = [room.take(P, D) for u in range(2)]
        routing = Room()
        place16 = routing.take(S, B, P, dt=F16)
        slot16 = routing.take(S, B, 2, COLS, dt=F16)

        bank = [stack.enter_context(nc.psum_tensor(f"bank{n}", [P, 512], F32)) for n in range(8)]

        def cols2(b, n=S):
            return bank[b][:, 0:DC * n].rearrange("p (c n) -> p c n", c=DC)

        names = """x0_in x_in xw_in0 xw_in1 ctx_in0 ctx_in1 wqk_in wv_in
            slope_in a_in m_in gate_in b1_in b2_raw_in ident_ready ones_ready
            alibi_flat alibi_ready wide_ready
            wvT_psum wvT_ready woT_psum woT_ready gwT_ready a_psum a_ready m_psum m_ready c_psum
            c_ready bx_psum bx_ready b1_ready b2_split b2_stored b2_in b2_zeroed
            stage_in0 stage_in1 stage_in2 stage_in3 hi_ready0 hi_ready1 hi_ready2 hi_ready3
            lo_ready0 lo_ready1 lo_ready2 lo_ready3
            xT_psum xT_ready gT_psum gT_ready sc_psum sc_biased sc_max p_ready p_inv pT_psum pT_ready
            uT_psum uT_ready out1_psum y1_ready y1_bn y1_agg y1_eps y1_rstd x1_ready x1b_ready
            x1T_psum x1T_ready rT_psum rT_ready cT_psum cT_ready sc2_psum sc2_max pc_ready pc_inv
            pcT_psum pcT_ready ccT_psum ccT_ready out2_psum y2_ready y2_bn y2_agg y2_eps y2_rstd x2_ready x2_stored
            x2T_psum x2T_ready gate_psum logit_ready
            route route2 hot_ready rank_psum table16_ready table_psum used_ready
            idx_ready0 idx_ready1 oidx_ready0 oidx_ready1 gathered0 gathered1 kept xgT_psum xgT_hi_ready xgT_lo_ready
            pre0_psum pre1_psum pre0_ready pre1_ready hT0_psum hT1_psum h0_ready h1_ready h2_ready h3_ready
            hi0_ready hi1_ready hi2_ready hi3_ready lo0_ready lo1_ready lo2_ready lo3_ready y3_psum y3_ready y3_bn y3_agg y3_eps y3_rstd o_ready
            scattered0 scattered1 passed""".split()
        s = {n: sem(n) for n in names}
        c_in = [s["ctx_in0"], s["ctx_in1"]]
        gathered = [s["gathered0"], s["gathered1"]]
        scattered = [s["scattered0"], s["scattered1"]]
        idx_ready = [s["idx_ready0"], s["idx_ready1"]]
        oidx_ready = [s["oidx_ready0"], s["oidx_ready1"]]

        def waited(e):
            e.sem_inc(s["passed"], 1)

        class Step:

            def __init__(self, t, u):
                self.t, self.u = t, u
                self.n = 2 * t + u
                self.a, self.b, self.c, self.d, self.g = (self.batch(k) for k in range(5))

            def batch(self, k):
                n = self.n - k
                return n if not isinstance(n, int) or 0 <= n < B else None

            def half(self, k):
                side = (self.u - k) % 2
                return side, self.t + (self.u - k - side) // 2

        STAGES = 5
        FIRST = 4
        assert FIRST + E == B + STAGES - 1

        def part(w, e, q):
            return w[:, bass.ds(e * WE + q * QW, QW)]

        def staged(q):
            return stage[:, q * QW:(q + 1) * QW]

        def has_expert(p):
            return not isinstance(p.n, int) or FIRST <= p.n < B + STAGES - 2

        def alone_d(p):
            return isinstance(p.n, int) and p.n == B + STAGES - 3

        def step_before(p):
            return Step((p.n - 1) // 2, (p.n - 1) % 2)

        def has_last_expert(p):
            return isinstance(p.n, int) and p.n == B + STAGES - 2

        FULL = -(-(STAGES - 1) // 2)
        FIRST_COPY = 2 * FULL - 1

        def run_steps(e, step, between=None):
            for n in range(2 * FULL):
                if between:
                    between(n)
                step(Step(n // 2, n % 2))
            with e.Fori(FULL, B // 2) as t:
                for u in range(2):
                    step(Step(t, u))
            for n in range(B, B + STAGES - 1):
                step(Step(n // 2, n % 2))

        def x_of(p, k):
            n = p.batch(k)
            return x_all[:, n, :] if isinstance(n, int) else xw[p.half(k)[0]][:, :]

        xw_in = [s["xw_in0"], s["xw_in1"]]

        def xw_loads(p, k):
            side, before = p.half(k)
            return before + 1 - (FIRST_COPY + 1 - side) // 2

        block = stack.enter_context(nc.Block())

        @block.sync
        def _(sp):
            def load_ctx(k, step):
                side, before = step.half(k)
                if not (isinstance(before, int) and before == 0):
                    sp.wait_ge(s["ccT_psum"], step.n - k - 1)
                sp.dma_start(cw[side].rearrange("p c d -> p (c d)"),
                             ctx_in[bass.ds(step.n - k, 1), :, :].rearrange("o (p c) d -> (o p) (c d)", c=KC)).then_inc(c_in[side], 16)

            def load_expert(e):
                if isinstance(e, int) and e == 0:
                    sp.wait_ge(s["bx_psum"], 1)
                    sp.wait_ge(s["m_psum"], 1)
                for q in (2, 0, 3, 1):
                    if not (isinstance(e, int) and e == 0):
                        sp.wait_ge(s[f"lo_ready{q}"], e)
                        sp.wait_ge(s[f"hi_ready{q}"], e)
                        waited(sp)
                    if q < 2:
                        src = w1[bass.ds(e, 1), q * P:(q + 1) * P, :].rearrange("o p f -> p (o f)")
                        sp.dma_start(staged(q), src).then_inc(s[f"stage_in{q}"], 16)
                    else:
                        h = q - 2
                        src = w2[bass.ds(e, 1), h * F // 2:(h + 1) * F // 2, :].rearrange("o (c p) d -> p (o c) d", p=P)
                        sp.dma_start(staged(q).rearrange("p (c d) -> p c d", d=D), src).then_inc(s[f"stage_in{q}"], 16)

            def load(name, dst, src):
                sp.dma_start(dst, src, allow_slow_non_contiguous=True).then_inc(s[name], 16)

            def load_weight(name, dst, src):
                load(name, dst, src.rearrange("(c p) e -> p c e", p=P))

            def load_x(p):
                n = p.batch(-1)
                side, _ = p.half(-1)
                if not (isinstance(n, int) and n < FIRST_COPY + 2):
                    sp.wait_ge(s["uT_psum"], n - 1)
                sp.dma_start(xw[side][:, :], x[bass.ds(n, 1), :, :].rearrange("o s d -> (o s) d")).then_inc(xw_in[side], 16)

            def step(p):
                if p.batch(-1) is not None and not (isinstance(p.n, int) and not FIRST_COPY <= p.n + 1 < B):
                    load_x(p)
                if p.g is not None:
                    sp.wait_ge(s["x2_ready"], p.g + 1)
                    sp.dma_start(x2_rows[bass.ds(p.g * S, S), :], x2[:, :]).then_inc(s["x2_stored"], 16)
                if p.batch(1) is not None and not (isinstance(p.n, int) and p.n < 3):
                    load_ctx(1, p)
                if not (isinstance(p.n, int) and p.n in (FIRST - 1 + E, *range(FIRST - 1))):
                    load_expert(p.n - FIRST + 1)

            sp.sem_inc(s["x2_stored"], 16)
            load("x0_in", x_all[:, 0, :], x[0])
            load_weight("wqk_in", wqk_s[:, :, :], w_qk)
            load("slope_in", slope_c[:, :], slope.partition_broadcast(S))
            load("x_in", x_all[:, 1:B, :], x[1:B].rearrange("b s d -> s b d"))
            load_weight("wv_in", raw_wv, w_v)
            load_weight("a_in", raw_wq, wq)
            load_weight("a_in", raw_wk, wk)
            load("a_in", bq_col[:, :], bq.rearrange("(c p) -> p c", p=P))
            load_ctx(0, Step(0, 0))
            load_weight("m_in", raw_wo, wo)
            load_weight("m_in", raw_xv, w_xv)
            load("m_in", bv_col[:, :], bv.rearrange("(c p) -> p c", p=P))
            load("m_in", bo_row[:, :], bo.rearrange("(o d) -> o d", o=1))
            load_ctx(0, Step(0, 1))
            load("gate_in", gw_raw[:, :], gate_w)
            load("gate_in", gb_raw[:, 0, :], gate_b.partition_broadcast(S))
            load("gate_in", gb_raw[:, 1, :], expert_bias.partition_broadcast(S))
            load("b1_in", b1_raw[:, :], b1.rearrange("e (c p) -> (e c) p", p=P))
            load("b2_raw_in", b2_raw[:, :], b2)
            for n in range(2 * FULL):
                step(Step(n // 2, n % 2))
            with sp.Fori(FULL, B // 2 - 1) as t:
                for u in range(2):
                    step(Step(t, u))
            for n in range(B - 2, B + STAGES - 1):
                step(Step(n // 2, n % 2))

        @block.gpsimd
        def _(pool):
            pool.memset(ident[:, :], 0.0).then_inc(s["ident_ready"], 1)
            pool.wait_ge(s["ident_ready"], 1)
            pool.affine_select(out=ident[:, :], in_=ident[:, :], compare_op=ALU.not_equal, fill=1.0, base=0,
                               pattern=[[-1, P]], channel_multiplier=1).then_inc(s["ident_ready"], 1)

            def rstd(n, k, rows):
                var = st[0:rows, 8 * n + 2:8 * n + 3]
                pool.wait_ge(s[f"y{n}_agg"], k + 1)
                pool.tensor_tensor(var, var, st[0:rows, 40:41], ALU.add).then_inc(s[f"y{n}_eps"], 1)
                pool.wait_ge(s[f"y{n}_eps"], k + 1)
                pool.tensor_tensor(var, var, st[0:rows, 41:42], ALU.pow).then_inc(s[f"y{n}_rstd"], 1)

            def split_lo(p, q):
                e = p.n - FIRST
                pool.wait_ge(s[f"hi_ready{q}"], e + 1)
                pool.wait_ge(s[f"stage_in{q}"], 16 * (e + 1))
                pool.tensor_tensor(part(w_lo, e, q), staged(q), part(w_hi, e, q), ALU.subtract).then_inc(s[f"lo_ready{q}"], 1)

            def add_bias(p):
                side, before = p.half(2)
                pool.wait_ge(s["x1_ready"], p.c + 1)
                if not (isinstance(before, int) and before == 0):
                    pool.wait_ge(s["y2_ready"], p.c - 1)
                pool.wait_ge(s["bx_ready"], 1)
                pool.tensor_tensor(x1b[side][:, :], x1[:, :], b_x[:, :], ALU.add).then_inc(s["x1b_ready"], 1)

            pool.iota(iota_i[:, 0:P], pattern=[[1, P]], base=0, channel_multiplier=-1).then_inc(s["ones_ready"], 1)
            pool.iota(iota_i[:, P:2 * P], pattern=[[1, P]], base=0, channel_multiplier=0).then_inc(s["ones_ready"], 1)
            pool.iota(iota_i[:, 2 * P:2 * P + B], pattern=[[S, B]], base=0, channel_multiplier=1).then_inc(s["ones_ready"], 1)
            pool.memset(st[:, 40:41], EPS).then_inc(s["ones_ready"], 1)
            pool.memset(st[:, 41:42], -0.5).then_inc(s["ones_ready"], 1)
            pool.memset(ones[:, :], 1.0).then_inc(s["ones_ready"], 1)
            pool.memset(ones3[:, :], 0.0).then_inc(s["ident_ready"], 1)
            pool.memset(ones16[:, :], 1.0).then_inc(s["ones_ready"], 1)
            pool.wait_ge(s["ident_ready"], 3)
            pool.memset(ones3[0:3, :], 1.0).then_inc(s["ones_ready"], 1)
            pool.wait_ge(s["ones_ready"], 8)
            pool.affine_select(out=low16[:, :], in_=ones16[:, :], compare_op=ALU.is_gt, fill=0.0, base=0,
                               pattern=[[1, P]], channel_multiplier=-1).then_inc(s["ones_ready"], 1)
            pool.wait_ge(s["alibi_flat"], 1)
            pool.affine_select(out=alibi[:, :], in_=alibi[:, :], compare_op=ALU.is_ge, fill=MASKED, base=0,
                               pattern=[[-1, S]], channel_multiplier=1).then_inc(s["alibi_ready"], 1)

            def step(p):
                if p.c is not None:
                    rstd(1, p.c, S)
                if p.g is not None:
                    rstd(2, p.g, S)
                if p.c is not None:
                    add_bias(p)
                if has_expert(p):
                    split_lo(p, 0)
                if has_expert(p) and not alone_d(p):
                    split_lo(p, 1)
                if isinstance(p.n, int) and p.n == B:
                    pool.wait_ge(s["b2_split"], 1)
                    pool.dma_start(b2_parts.rearrange("n e d -> e n d"), b2_split[:, :, :]).then_inc(s["b2_stored"], 16)
                if has_last_expert(p):
                    pool.wait_ge(s["b2_stored"], 16)
                    pool.wait_ge(s["b2_zeroed"], 1)
                    pool.dma_start(b2_rows[0:3, :], b2_parts.rearrange("n e d -> n (e d)")).then_inc(s["b2_in"], 16)
                    split_lo(step_before(p), 1)
                    for q in (2, 0):
                        split_lo(p, q)

            pool.memset(b2_rows[:, :].bitcast(F32), 0.0).then_inc(s["b2_zeroed"], 1)
            run_steps(pool, step)

            last_row = pool.to_reg(N - 1)

            def gather(u, k):
                pool.wait_ge(idx_ready[u], k + 1)
                waited(pool)
                pool.indirect_dma_start(xg[u], None, x2_rows, bass.IndirectOffsetOnAxis(ap=idx_in[u][:, :].bitcast(U32), axis=0),
                                        bounds_check=last_row, oob_is_err=False).then_inc(gathered[u], 16)

            def rows_in(t, u):
                n = 2 * t + u
                pool.wait_ge(gathered[u], 16 * (t + 1))
                pool.wait_ge(s["y3_ready"], n + 1)
                waited(pool)
                pool.tensor_scalar(x_keep[u], xg[u], 1.0, 0.0, ALU.mult, ALU.add).then_inc(s["kept"], 1)
                pool.wait_ge(s["kept"], n + 1)
                pool.wait_ge(s["xgT_psum"], n + 1)
                gather(u, t + 1)

            def rows_out(t, u):
                pool.wait_ge(s["o_ready"], 2 * t + u + 1)
                pool.wait_ge(oidx_ready[u], t + 1)
                waited(pool)
                pool.indirect_dma_start(out.rearrange("b s d -> (b s) d"),
                                        bass.IndirectOffsetOnAxis(ap=idx_out[u][:, :].bitcast(U32), axis=0),
                                        y3n[u], None, bounds_check=last_row, oob_is_err=False).then_inc(scattered[u], 16)

            pool.wait_ge(s["x2_stored"], 16 * (B + 1))
            gather(0, 0)
            gather(1, 0)
            pool.wait_ge(s["used_ready"], 2)
            used = pool.value_load(slots_used[0:1, 0:1], min_val=TILES, max_val=SLOTS)
            for u in range(2):
                rows_in(0, u)
            with pool.Fori(1, SLOTS // 2 + 1) as t:
                for u in range(2):
                    n = 2 * t + u
                    with pool.If(n < used + 2):
                        rstd(3, n - 2, P)
                    with pool.If(n < used):
                        rows_in(t, u)
                    with pool.If(n < used + 2):
                        rows_out(t - 1, u)
            for u in range(2):
                slots = (used + 1 - u) // 2
                pool.wait_ge(scattered[u], 16 * slots)
                pool.wait_ge(gathered[u], 16 * (slots + 1))

        @block.scalar
        def _(act):
            def copy(dst, src, scale=1.0):
                return act.activation(dst, src, ACT.Copy, scale=scale)

            def split_hi(p, q):
                e = p.n - FIRST
                act.wait_ge(s[f"stage_in{q}"], 16 * (e + 1))
                copy(part(w_hi, e, q), staged(q)).then_inc(s[f"hi_ready{q}"], 1)

            def step(p):
                if p.b is not None:
                    act.wait_ge(s["pT_psum"], p.b + 1)
                    copy(pT[:, :], bank[1][0:S, 0:S]).then_inc(s["pT_ready"], 1)
                if p.d is not None:
                    act.wait_ge(s["pcT_psum"], p.d + 1)
                    copy(pcT[:, :, :], bank[2][0:SP_, 0:KC * S].rearrange("p (c n) -> p c n", c=KC)).then_inc(s["pcT_ready"], 1)
                if p.a is not None:
                    act.wait_ge(s["xT_psum"], p.a + 1)
                    copy(xT[:, :, :], cols2(0)).then_inc(s["xT_ready"], 1)
                if p.b is not None:
                    act.wait_ge(s["uT_psum"], p.b + 1)
                    copy(uT[:, :, :], cols2(4)).then_inc(s["uT_ready"], 1)
                if has_expert(p) and p.a is not None:
                    split_hi(p, 2)
                if p.d is not None:
                    act.wait_ge(s["ccT_psum"], p.d + 1)
                    copy(ccT[:, :, :], cols2(1)).then_inc(s["ccT_ready"], 1)
                if has_expert(p) and p.a is None:
                    split_hi(p, 2)
                if p.c is not None:
                    act.wait_ge(s["x1T_psum"], p.c + 1)
                    copy(x1T[:, :, :], cols2(3)).then_inc(s["x1T_ready"], 1)
                if p.a is not None:
                    act.wait_ge(s["gT_psum"], p.a + 1)
                    copy(gT[:, :, :], cols2(0), SCALE).then_inc(s["gT_ready"], 1)
                if p.g is not None:
                    act.wait_ge(s["x2T_psum"], p.g + 1)
                    copy(x2T[:, :, :], cols2(7)).then_inc(s["x2T_ready"], 1)
                if p.c is not None:
                    act.wait_ge(s["cT_psum"], p.c + 1)
                    copy(cT[:, 0, :], bank[5][:, 0:SK]).then_inc(s["cT_ready"], 1)
                if p.c is not None:
                    act.wait_ge(s["rT_psum"], p.c + 1)
                    act.wait_ge(s["c_ready"], 1)
                    for d in range(DC):
                        act.activation(rT[:, d, :], cols2(2)[:, d, :], ACT.Identity, bias=c_x[:, d:d + 1]).then_inc(s["rT_ready"], 1)
                if p.a is not None:
                    act.wait_ge(s["sc_max"], p.a + 1)
                    act.activation(pr[:, :], sc[:, :], ACT.Exp, bias=st[0:S, 0:1], accum_out=st[0:S, 1:2]).then_inc(s["p_ready"], 1)
                if has_expert(p):
                    split_hi(p, 1)
                if p.c is not None:
                    act.wait_ge(s["sc2_max"], p.c + 1)
                    act.activation(pc[:, :], bank[5][0:S, 0:SK], ACT.Exp, bias=st[0:S, 2:3], accum_out=st[0:S, 3:4]).then_inc(s["pc_ready"], 1)
                if has_last_expert(p):
                    for q in (2, 0, 3, 1):
                        split_hi(p, q)

            def between(n):
                if n == 1:
                    act.wait_ge(s["wvT_psum"], 1)
                    copy(wvT[:, :, :], bank[7][:, :].rearrange("p (c d) -> p c d", c=DC)).then_inc(s["wvT_ready"], 1)
                if n == 2:
                    act.wait_ge(s["a_psum"], 1)
                    copy(a_x[:, :, :], bank[6][:, :].rearrange("p (c d) -> p c d", c=DC), SCALE).then_inc(s["a_ready"], 1)
                    act.wait_ge(s["c_psum"], 1)
                    copy(c_x[:, :], bank[5][:, 0:DC], SCALE).then_inc(s["c_ready"], 1)
                    act.wait_ge(s["woT_psum"], 1)
                    copy(woT, bank[7][:, :].rearrange("p (c d) -> p c d", c=DC)).then_inc(s["woT_ready"], 1)
                if n == 3:
                    act.wait_ge(s["bx_psum"], 1)
                    copy(b_x[:, :], bank[7][0:S, 0:D]).then_inc(s["bx_ready"], 1)
                    copy(gwT[:, :, :], bank[7][:, D:D + DC * E].rearrange("p (c d) -> p c d", c=DC)).then_inc(s["gwT_ready"], 1)
                    copy(b1T[:, :], bank[7][:, D + DC * E:D + DC * E + E * FC]).then_inc(s["b1_ready"], 1)
                    act.wait_ge(s["m_psum"], 1)
                    copy(m_x[:, :, :], bank[6][:, :].rearrange("p (c d) -> p c d", c=DC)).then_inc(s["m_ready"], 1)

            run_steps(act, step, between)

            def rows_hi(n, u):
                act.wait_ge(s["xgT_psum"], n + 1)
                copy(xgT_hi[u], cols2(6, P)).then_inc(s["xgT_hi_ready"], 1)

            rows_hi(0, 0)
            act.wait_ge(s["b1_ready"], 1)
            act.wait_ge(s["used_ready"], 2)
            used = act.value_load(slots_used[0:1, 0:1], min_val=TILES, max_val=SLOTS)
            with act.Fori(0, SLOTS // 2) as t:
                for u in range(2):
                    n = 2 * t + u
                    with act.If(n < used):
                        e = act.value_load(slot_expert[0:1, bass.ds(n, 1)], min_val=0, max_val=E - 1)
                        for h in range(2):
                            act.wait_ge(s[f"pre{h}_psum"], n + 1)
                            copy(pre[:, h * FH:(h + 1) * FH], bank[h][:, :]).then_inc(s[f"pre{h}_ready"], 1)
                        for h in range(2):
                            act.wait_ge(s[f"hT{h}_psum"], n + 1)
                            for k in range(FC // 2):
                                c = h * FC // 2 + k
                                last = act.activation(hid[:, c * P:(c + 1) * P], bank[2 + h][:, k * P:(k + 1) * P], ACT.Relu,
                                                      bias=b1T[:, bass.ds(e * FC + c, 1)])
                                if k % 2 == 1:
                                    last.then_inc(s[f"h{c // 2}_ready"], 1)
                                if c == 1:
                                    rows_hi(n + 1, 1 - u)

        @block.vector
        def _(dve):
            done = [0]

            def link(ins):
                done[0] += 1
                ins.then_inc(s["route"], 1)
                dve.wait_ge(s["route"], done[0])

            dve.wait_ge(s["ones_ready"], 9)
            dve.wait_ge(s["slope_in"], 16)
            dve.tensor_copy(num[:, :], iota_i[0:S, P:2 * P])
            dve.tensor_copy(num16[:, :], iota_i[0:S, P:2 * P])
            link(dve.tensor_copy(sc[:, :], iota_i[0:S, 0:S]))
            dve.tensor_scalar(alibi[:, :], sc[:, :], slope_c[:, 0:1], None, ALU.mult).then_inc(s["alibi_flat"], 1)

            sizes = [B, E, TILES, E * E]
            token, back, bound, earlier = (route_consts[:, sum(sizes[:k]):sum(sizes[:k + 1])] for k in range(4))
            earlier = earlier.rearrange("p (a b) -> p a b", b=E)

            def rows(v, n):
                return v.unsqueeze(1).to_broadcast([S, n, v.shape[-1]])

            def cols(v, n):
                return v.unsqueeze(2).to_broadcast([S, v.shape[-1], n])

            dve.tensor_copy(token, iota_i[0:S, 2 * P:2 * P + B])
            dve.tensor_scalar(back, num[:, 0:E], -1.0, float(E), ALU.mult, ALU.add)
            dve.tensor_scalar(bound, num[:, 0:TILES], float(P), None, ALU.mult)
            link(dve.tensor_tensor(earlier, rows(num[:, 0:E], E), cols(num[:, 0:E], E), ALU.is_lt))

            def ln_mean(n, y, rows, k):
                part = st[0:rows, 38 + 6 * n:44 + 6 * n]
                dve.wait_ge(s[f"y{n}_ready"], k + 1 + 2 * (n == 3))
                dve.bn_stats(part, y).then_inc(s[f"y{n}_bn"], 1)

            def ln_merge(n, rows, k):
                part = st[0:rows, 38 + 6 * n:44 + 6 * n]
                dve.wait_ge(s[f"y{n}_bn"], k + 1)
                waited(dve)
                dve.bn_aggr(st[0:rows, 8 * n + 1:8 * n + 3], part).then_inc(s[f"y{n}_agg"], 1)

            def ln_apply(n, dst, y, rows, k):
                dve.wait_ge(s[f"y{n}_rstd"], k + 1)
                return dve.tensor_scalar(dst, y, st[0:rows, 8 * n + 1:8 * n + 2], st[0:rows, 8 * n + 2:8 * n + 3],
                                         ALU.subtract, ALU.mult)

            def split_hi(p, q):
                e = p.n - FIRST
                dve.wait_ge(s[f"stage_in{q}"], 16 * (e + 1))
                dve.tensor_copy(part(w_hi, e, q), staged(q)).then_inc(s[f"hi_ready{q}"], 1)

            def split_lo(p, q):
                e = p.n - FIRST
                dve.wait_ge(s[f"hi_ready{q}"], e + 1)
                dve.wait_ge(s[f"stage_in{q}"], 16 * (e + 1))
                dve.tensor_tensor(part(w_lo, e, q), staged(q), part(w_hi, e, q), ALU.subtract).then_inc(s[f"lo_ready{q}"], 1)

            def step(p):
                if p.c is not None:
                    if not (isinstance(p.c, int) and p.c == 0):
                        dve.wait_ge(s["x1b_ready"], p.c)
                    ln_apply(1, x1[:, :], y1[:, :], S, p.c).then_inc(s["x1_ready"], 1)
                if p.g is not None:
                    dve.wait_ge(s["x2_stored"], 16 * p.g + 16)
                    ln_apply(2, x2[:, :], y2[:, :], S, p.g).then_inc(s["x2_ready"], 1)
                if p.b is not None:
                    dve.wait_ge(s["p_ready"], p.b + 1)
                    dve.reciprocal(st[0:S, 4:5], st[0:S, 1:2]).then_inc(s["p_inv"], 1)
                if p.d is not None:
                    dve.wait_ge(s["pc_ready"], p.d + 1)
                    dve.reciprocal(st[0:S, 5:6], st[0:S, 3:4]).then_inc(s["pc_inv"], 1)
                if has_last_expert(p):
                    split_lo(step_before(p), 3)
                if has_expert(p):
                    split_hi(p, 0)
                    split_hi(p, 3)
                if has_expert(p) and not alone_d(p):
                    split_lo(p, 2)
                if p.c is not None:
                    dve.wait_ge(s["cT_psum"], p.c + 1)
                    dve.tensor_copy(cT[:, 1, :], bank[6][:, 0:SK]).then_inc(s["cT_ready"], 1)
                if p.a is not None:
                    dve.wait_ge(s["sc_psum"], p.a + 1)
                    dve.wait_ge(s["alibi_ready"], 1)
                    dve.tensor_tensor(sc[:, :], bank[3][0:S, 0:S], alibi[:, :], ALU.add).then_inc(s["sc_biased"], 1)
                    dve.wait_ge(s["sc_biased"], p.a + 1)
                    dve.tensor_reduce(st[0:S, 0:1], sc[:, :], AX.X, ALU.max, negate=True).then_inc(s["sc_max"], 1)
                if has_expert(p) and not alone_d(p):
                    split_lo(p, 3)
                if p.g is not None:
                    dve.wait_ge(s["gate_psum"], p.g + 1)
                    dve.wait_ge(s["logit_ready"], 1)
                    dve.tensor_tensor(logit[:, bass.ds(p.g, 1), :].rearrange("p o e -> p (o e)"), bank[7][0:S, 0:E],
                                      gb[:, :], ALU.add).then_inc(s["logit_ready"], 1)
                if p.c is not None:
                    dve.wait_ge(s["sc2_psum"], p.c + 1)
                    dve.tensor_reduce(st[0:S, 2:3], bank[5][0:S, 0:SK], AX.X, ALU.max, negate=True).then_inc(s["sc2_max"], 1)
                if p.b is not None:
                    dve.wait_ge(s["out1_psum"], p.b + 1)
                    dve.wait_ge(s["p_inv"], p.b + 1)
                    dve.wait_ge(s["x0_in"], 16)
                    dve.wait_ge(s["x_in"], 16)
                    dve.scalar_tensor_tensor(y1[:, :], bank[4][0:S, 0:D], st[0:S, 4:5],
                                             x_all[:, bass.ds(p.b, 1), :].rearrange("p o d -> p (o d)"),
                                             ALU.mult, ALU.add).then_inc(s["y1_ready"], 1)
                    ln_mean(1, y1[:, :], S, p.b)
                    ln_merge(1, S, p.b)
                if p.d is not None:
                    dve.wait_ge(s["out2_psum"], p.d + 1)
                    dve.wait_ge(s["pc_inv"], p.d + 1)
                    dve.wait_ge(s["x1b_ready"], p.d + 1)
                    dve.scalar_tensor_tensor(y2[:, :], bank[6][0:S, 0:D], st[0:S, 5:6], x1b[p.half(3)[0]][:, :],
                                             ALU.mult, ALU.add).then_inc(s["y2_ready"], 1)
                    ln_mean(2, y2[:, :], S, p.d)
                    ln_merge(2, S, p.d)
                if alone_d(p):
                    split_lo(p, 2)

            def between(n):
                if n == 1:
                    dve.wait_ge(s["m_in"], 16 * 4)
                    dve.tensor_copy(bv_wide[:, :, :], bv_col[:, :].unsqueeze(2).to_broadcast([P, DC, S])).then_inc(s["wide_ready"], 1)
                    dve.wait_ge(s["gate_in"], 16 * 3)
                    dve.tensor_tensor(gb[:, :], gb_raw[:, 0, :], gb_raw[:, 1, :], ALU.add).then_inc(s["logit_ready"], 1)
                if n != 2:
                    return
                dve.wait_ge(s["b2_raw_in"], 16)
                hi, mid, low = (b2_split[:, n, :] for n in range(3))
                link(dve.tensor_copy(hi, b2_raw[:, :]))
                link(dve.tensor_tensor(b2_raw[:, :], b2_raw[:, :], hi, ALU.subtract))
                link(dve.tensor_copy(mid, b2_raw[:, :]))
                link(dve.tensor_tensor(b2_raw[:, :], b2_raw[:, :], mid, ALU.subtract))
                dve.tensor_copy(low, b2_raw[:, :]).then_inc(s["b2_split"], 1)

            run_steps(dve, step, between)

            def room(*shape):
                v = routing.take(S, *shape)
                assert routing.at <= routing_end
                return v

            order = [0]

            def do(ins):
                order[0] += 1
                ins.then_inc(s["route2"], 1)
                return order[0]

            def need(n):
                dve.wait_ge(s["route2"], n)

            top = room(B)
            hot = room(B, E)
            pick = room(B)
            dve.wait_ge(s["logit_ready"], B + 1)
            need(do(dve.tensor_reduce(top, logit[:, :, :], AX.X, ALU.max)))
            need(do(dve.tensor_tensor(hot, logit[:, :, :], cols(top, E), ALU.is_equal)))
            need(do(dve.tensor_tensor(hot, hot, rows(back, B), ALU.mult)))
            need(do(dve.tensor_reduce(pick, hot, AX.X, ALU.max)))
            dve.tensor_tensor(oh16[:, :, :], cols(pick, E), rows(back, B), ALU.is_equal).then_inc(s["hot_ready"], 1)
            is_hot = do(dve.tensor_tensor(hot, cols(pick, E), rows(back, B), ALU.is_equal))

            more = room(E, TILES)
            tiles = room(E)
            before = room(E, E)
            first = room(E)
            rank = room(B, E)
            mine = room(B)
            over = room(B, TILES - 1)
            tile = room(B)
            place = room(B)
            base = room(B)
            slot = room(B)
            dve.wait_ge(s["rank_psum"], 1)
            a = do(dve.tensor_tensor(more, cols(bank[1][0:S, 0:E], TILES), rows(bound, E), ALU.is_gt))
            need(is_hot)
            b = do(dve.tensor_tensor(rank, hot, bank[0][0:S, 0:B * E].rearrange("p (b e) -> p b e", e=E), ALU.mult))
            need(a)
            a = do(dve.tensor_reduce(tiles, more, AX.X, ALU.add))
            need(b)
            b = do(dve.tensor_reduce(mine, rank, AX.X, ALU.add))
            need(a)
            a = do(dve.tensor_tensor(before, earlier, rows(tiles, E), ALU.mult))
            need(b)
            b = do(dve.tensor_tensor(over, cols(mine, TILES - 1), rows(bound[:, 1:TILES], B), ALU.is_ge))
            need(a)
            a = do(dve.tensor_reduce(first, before, AX.X, ALU.add))
            need(b)
            b = do(dve.tensor_reduce(tile, over, AX.X, ALU.add))
            need(a)
            a = do(dve.tensor_tensor(rank, hot, rows(first, B), ALU.mult))
            need(b)
            b = do(dve.scalar_tensor_tensor(place, tile, -float(P), mine, ALU.mult, ALU.add))
            need(a)
            a = do(dve.tensor_reduce(base, rank, AX.X, ALU.add))
            need(b)
            for k in range(B // 2):
                dve.tensor_scalar(place16[:, k, :], num16[:, :], place[:, k:k + 1], None, ALU.is_equal)
            need(a)
            a = do(dve.tensor_tensor(slot, base, tile, ALU.add))
            for k in range(B // 2, B):
                dve.tensor_scalar(place16[:, k, :], num16[:, :], place[:, k:k + 1], None, ALU.is_equal)
            need(a)
            need(do(dve.tensor_tensor(slot16[:, :, 1, :], rows(num[:, 0:COLS], B), cols(slot, COLS), ALU.is_equal)))
            dve.tensor_tensor(slot16[:, :, 0, :], slot16[:, :, 1, :], cols(token, COLS), ALU.mult).then_inc(s["table16_ready"], 1)
            starts = room(COLS, E - 1)
            owner = room(COLS)
            total = room(1)
            a = do(dve.tensor_tensor(starts, cols(num[:, 0:COLS], E - 1), rows(first[:, 1:E], COLS), ALU.is_ge))
            b = do(dve.tensor_reduce(total, tiles, AX.X, ALU.add))
            need(a)
            a = do(dve.tensor_reduce(owner, starts, AX.X, ALU.add))
            need(b)
            dve.tensor_copy(slots_used[:, 0:1], total[0:1, :]).then_inc(s["used_ready"], 1)
            need(a)
            dve.tensor_copy(slot_expert[:, :], owner[0:1, :]).then_inc(s["used_ready"], 1)
            both = owner[0:1, :].rearrange("p (t u) -> p t u", u=2)
            dve.scalar_tensor_tensor(pair_experts[:, :], both[:, :, 1], float(E), both[:, :, 0], ALU.mult, ALU.add).then_inc(s["used_ready"], 1)

            dve.wait_ge(s["table_psum"], 1)
            for u in range(2):
                dve.tensor_copy(idx_in[u][:, :], bank[7][:, u:u + 1]).then_inc(idx_ready[u], 1)
            unused = y3[:, 0:COLS]
            need(do(dve.tensor_scalar(unused, bank[7][:, COLS:2 * COLS], -float(DROP), float(DROP), ALU.mult, ALU.add)))
            do(dve.tensor_copy(row_in[:, :], bank[7][:, 0:COLS]))
            need(do(dve.tensor_tensor(row_out[:, :], bank[7][:, 0:COLS], unused, ALU.add)))

            for q in (3, 1):
                split_lo(Step((B + STAGES - 2) // 2, (B + STAGES - 2) % 2), q)

            dve.sem_inc(s["y3_ready"], 2)

            def rows_lo(n, u):
                dve.wait_ge(s["xgT_hi_ready"], n + 1)
                dve.tensor_tensor(xgT_lo[u], cols2(6, P), xgT_hi[u], ALU.subtract).then_inc(s["xgT_lo_ready"], 1)

            def split_hidden(n, u, q):
                at = slice(q * QF, (q + 1) * QF)
                dve.wait_ge(s[f"h{q}_ready"], n + 1)
                dve.tensor_copy(hid_hi[u][:, at], hid[:, at]).then_inc(s[f"hi{q}_ready"], 1)
                dve.wait_ge(s[f"hi{q}_ready"], n + 1)
                dve.tensor_tensor(hid_lo[u][:, at], hid[:, at], hid_hi[u][:, at], ALU.subtract).then_inc(s[f"lo{q}_ready"], 1)

            def first_half(n, u):
                dve.tensor_copy(idx_in[u][:, :], row_in[:, bass.ds(n + 2, 1)]).then_inc(idx_ready[u], 1)
                split_hidden(n, u, 0)
                rows_lo(n + 1, 1 - u)
                split_hidden(n, u, 1)

            def second_half(n, u):
                split_hidden(n, u, 2)
                split_hidden(n, u, 3)

            def residual(n, u, t):
                if not (isinstance(t, int) and t == 0):
                    dve.wait_ge(scattered[u], 16 * t)
                dve.tensor_copy(idx_out[u][:, :], row_out[:, bass.ds(n, 1)]).then_inc(oidx_ready[u], 1)
                if not (isinstance(n, int) and n == 0):
                    dve.wait_ge(s["o_ready"], n)
                dve.wait_ge(s["kept"], n + 1)
                dve.wait_ge(s["y3_psum"], n + 1)
                dve.tensor_tensor(y3, bank[4 + u][:, 0:D], x_keep[u], ALU.add).then_inc(s["y3_ready"], 1)
                ln_mean(3, y3, P, n)
                ln_merge(3, P, n)

            rows_lo(0, 0)
            dve.wait_ge(s["used_ready"], 2)
            used = dve.value_load(slots_used[0:1, 0:1], min_val=TILES, max_val=SLOTS)
            for u in range(2):
                first_half(u, u)
                second_half(u, u)
                if u == 1:
                    residual(0, 0, 0)
            with dve.Fori(1, SLOTS // 2 + 1) as t:
                for u in range(2):
                    n = 2 * t + u
                    with dve.If(n < used):
                        first_half(n, u)
                    with dve.If(n < used + 2):
                        ln_apply(3, y3n[u], y3, P, n - 2).then_inc(s["o_ready"], 1)
                    with dve.If(n < used):
                        second_half(n, u)
                    with dve.If(n < used + 1):
                        residual(n - 1, 1 - u, t - 1 + u)

        @block.tensor
        def _(pe):
            def mm(dst, lhsT, rhs, k, last):
                return pe.matmul(dst, lhsT, rhs, start=(k == 0), stop=(k == last))

            def project(dst, weights, act_T):
                for e in range(DC):
                    for d in range(DC):
                        last = mm(dst[:, e, :], weights[:, d, e * P:(e + 1) * P], act_T[:, d, :], d, DC - 1)
                return last

            def flip(b, src, rows):
                for d in range(DC):
                    last = pe.transpose(cols2(b, rows)[:, d, :], src[:, d * P:(d + 1) * P], ident[0:rows, 0:rows])
                return last

            def flip_weights(b, src):
                dst = bank[b][:, :].rearrange("p (c d) -> p c d", c=DC)
                for d in range(DC):
                    for e in range(DC):
                        last = pe.transpose(dst[:, d, e * P:(e + 1) * P], src[:, e, d * P:(d + 1) * P], ident[:, :])
                return last

            def cross_output(p):
                pe.wait_ge(s["ccT_ready"], p.d + 1)
                for d in range(DC):
                    last = mm(bank[6][0:S, 0:D], ccT[:, d, :], m_x[:, d, :], d, DC - 1)
                last.then_inc(s["out2_psum"], 1)

            def step(p):
                if p.b is not None:
                    pe.wait_ge(s["p_ready"], p.b + 1)
                    pe.transpose(bank[1][0:S, 0:S], pr[:, :], ident[0:S, 0:S]).then_inc(s["pT_psum"], 1)
                if p.d is not None:
                    pe.wait_ge(s["pc_ready"], p.d + 1)
                    for k in range(KC):
                        last = pe.transpose(bank[2][0:SP_, k * S:(k + 1) * S], pc[:, k * SP_:(k + 1) * SP_], ident[0:S, 0:S])
                    last.then_inc(s["pcT_psum"], 1)
                if p.a is not None:
                    if isinstance(p.a, int):
                        pe.wait_ge(s["x_in" if p.a else "x0_in"], 16)
                    else:
                        pe.wait_ge(xw_in[p.half(0)[0]], 16 * xw_loads(p, 0))
                    flip(0, x_of(p, 0), S).then_inc(s["xT_psum"], 1)
                if p.b is not None:
                    pe.wait_ge(s["pT_ready"], p.b + 1)
                    if not isinstance(p.b, int):
                        pe.wait_ge(xw_in[p.half(1)[0]], 16 * xw_loads(p, 1))
                    if not (isinstance(p.b, int) and p.b == 0):
                        pe.wait_ge(s["y1_ready"], p.b)
                    for d in range(DC):
                        last = mm(cols2(4)[:, d, :], x_of(p, 1)[:, d * P:(d + 1) * P], pT[:, :], 0, 0)
                    last.then_inc(s["uT_psum"], 1)
                if p.d is not None:
                    side, _ = p.half(3)
                    pe.wait_ge(s["pcT_ready"], p.d + 1)
                    for d in range(DC):
                        for k in range(KC):
                            last = mm(cols2(1)[:, d, :], cw[side][:, k, d * P:(d + 1) * P], pcT[:, k, :], k, KC - 1)
                    last.then_inc(s["ccT_psum"], 1)
                if p.c is not None:
                    side, before = p.half(2)
                    pe.wait_ge(c_in[side], 16 * (before + 1))
                    if isinstance(p.c, int) and p.c < 2:
                        for name in ("m_ready",) if p.c else ("a_ready", "c_ready"):
                            pe.wait_ge(s[name], 1)
                    if not (isinstance(p.d, int) or p.d is None) or (isinstance(p.d, int) and p.d > 0):
                        pe.wait_ge(s["y2_ready"], p.d)
                    for d in range(DC):
                        for k in range(KC):
                            last = pe.transpose(bank[5 + d][:, k * SP_:(k + 1) * SP_], cw[side][:, k, d * P:(d + 1) * P], ident[0:SP_, 0:SP_])
                    last.then_inc(s["cT_psum"], 1)
                if p.c is not None:
                    pe.wait_ge(s["x1_ready"], p.c + 1)
                    pe.wait_ge(s["sc_biased"], p.c + 2 if p.batch(1) is not None else B)
                    flip(3, x1, S).then_inc(s["x1T_psum"], 1)
                if p.a is not None:
                    pe.wait_ge(s["xT_ready"], p.a + 1)
                    pe.wait_ge(s["wqk_in"], 16)
                    project(cols2(0), wqk_s, xT).then_inc(s["gT_psum"], 1)
                if p.g is not None:
                    pe.wait_ge(s["x2_ready"], p.g + 1)
                    pe.wait_ge(s["b1_ready"], 1)
                    pe.wait_ge(s["logit_ready"], p.g + 1)
                    flip(7, x2, S).then_inc(s["x2T_psum"], 1)
                if p.c is not None:
                    pe.wait_ge(s["x1T_ready"], p.c + 1)
                    project(cols2(2), a_x, x1T).then_inc(s["rT_psum"], 1)
                if p.a is not None:
                    pe.wait_ge(s["gT_ready"], p.a + 1)
                    for d in range(DC):
                        last = mm(bank[3][0:S, 0:S], gT[:, d, :], xT[:, d, :], d, DC - 1)
                    last.then_inc(s["sc_psum"], 1)
                if alone_d(p):
                    cross_output(p)
                if p.g is not None:
                    pe.wait_ge(s["x2T_ready"], p.g + 1)
                    pe.wait_ge(s["gwT_ready"], 1)
                    for d in range(DC):
                        last = mm(bank[7][0:S, 0:E], x2T[:, d, :], gwT[:, d, :], d, DC - 1)
                    last.then_inc(s["gate_psum"], 1)
                if p.b is not None:
                    pe.wait_ge(s["uT_ready"], p.b + 1)
                    if isinstance(p.b, int) and p.b == 0:
                        pe.wait_ge(s["wvT_ready"], 1)
                    for d in range(DC):
                        last = mm(bank[4][0:S, 0:D], uT[:, d, :], wvT[:, d, :], d, DC - 1)
                    last.then_inc(s["out1_psum"], 1)
                if p.c is not None:
                    pe.wait_ge(s["rT_ready"], DC * (p.c + 1))
                    pe.wait_ge(s["cT_ready"], DC * (p.c + 1))
                    for d in range(DC):
                        last = mm(bank[5][0:S, 0:SK], rT[:, d, :], cT[:, d, :], d, DC - 1)
                    last.then_inc(s["sc2_psum"], 1)
                if p.d is not None and not alone_d(p):
                    cross_output(p)

            def between(n):
                if n == 1:
                    pe.wait_ge(s["wv_in"], 16)
                    flip_weights(7, raw_wv).then_inc(s["wvT_psum"], 1)
                if n == 2:
                    pe.wait_ge(s["a_in"], 16 * 3)
                    for d in range(DC):
                        for e in range(DC):
                            last = mm(bank[6][:, d * D:(d + 1) * D], raw_wq[:, e, d * P:(d + 1) * P], raw_wk[:, e, :], e, DC - 1)
                    last.then_inc(s["a_psum"], 1)
                    for d in range(DC):
                        for e in range(DC):
                            last = mm(bank[5][:, d:d + 1], raw_wk[:, e, d * P:(d + 1) * P], bq_col[:, e:e + 1], e, DC - 1)
                    last.then_inc(s["c_psum"], 1)
                    pe.wait_ge(s["m_in"], 16 * 4)
                    flip_weights(7, raw_wo).then_inc(s["woT_psum"], 1)
                if n == 3:
                    pe.wait_ge(s["woT_ready"], 1)
                    pe.wait_ge(s["gate_in"], 16 * 3)
                    for d in range(DC):
                        last = pe.transpose(bank[7][:, D + d * E:D + (d + 1) * E], gw_raw[:, d * P:(d + 1) * P], ident[0:E, 0:E])
                    pe.wait_ge(s["b1_in"], 16)
                    pe.transpose(bank[7][:, D + DC * E:D + DC * E + E * FC], b1_raw[:, :], ident[0:E * FC, 0:E * FC])
                    pe.wait_ge(s["wide_ready"], 1)
                    pe.wait_ge(s["ones_ready"], 9)
                    for e in range(DC):
                        mm(bank[7][0:S, 0:D], bv_wide[:, e, :], woT[:, e, :], e, DC)
                    mm(bank[7][0:S, 0:D], ones[0:1, 0:S], bo_row[:, :], DC, DC).then_inc(s["bx_psum"], 1)
                    for d in range(DC):
                        for e in range(DC):
                            last = mm(bank[6][:, d * D:(d + 1) * D], raw_xv[:, e, d * P:(d + 1) * P], woT[:, e, :], e, DC - 1)
                    last.then_inc(s["m_psum"], 1)

            def warm_up(products):
                for _ in range(products):
                    pe.transpose(bank[4][:, 0:P], ident[:, :], ident[:, :])

            pe.wait_ge(s["ident_ready"], 2)
            warm_up(WARM)
            run_steps(pe, step, between)

            pe.wait_ge(s["hot_ready"], 1)
            for b in range(B - 1):
                pe.matmul(bank[0][:, (b + 1) * E:B * E], ones16[:, :],
                          oh16[:, b:b + 1, :].to_broadcast([S, B - 1 - b, E]), start=(b == 0), stop=False, skip_group_check=True)
            pe.matmul(bank[0][:, 0:B * E], low16[:, :], oh16[:, :, :].rearrange("p b e -> p (b e)"),
                      start=False, stop=True, skip_group_check=True)
            for b in range(B):
                last = mm(bank[1][:, 0:E], ones16[:, :], oh16[:, b, :], b, B - 1)
            last.then_inc(s["rank_psum"], 1)
            pe.wait_ge(s["table16_ready"], 1)
            for b in range(B):
                last = mm(bank[7][:, 0:2 * COLS], place16[:, b, :], slot16[:, b, :, :].rearrange("p t c -> p (t c)"), b, B - 1)
            last.then_inc(s["table_psum"], 1)
            warm_up(WARM)

            def flip_rows(u, k):
                pe.wait_ge(gathered[u], 16 * (k + 1))
                flip(6, xg[u], P).then_inc(s["xgT_psum"], 1)

            pe.wait_ge(s["used_ready"], 3)
            pe.wait_ge(s["b2_in"], 16)
            for q in range(4):
                pe.wait_ge(s[f"hi_ready{q}"], E)
                pe.wait_ge(s[f"lo_ready{q}"], E)
            used = pe.value_load(slots_used[0:1, 0:1], min_val=TILES, max_val=SLOTS)
            flip_rows(0, 0)

            def first_product(e, u, h):
                for d in range(DC):
                    at = bass.ds(e * WE + d * F + h * FH, FH)
                    pe.matmul(bank[h][:, :], xgT_hi[u][:, d, :], w_hi[:, at], start=(d == 0), stop=False)
                    pe.matmul(bank[h][:, :], xgT_lo[u][:, d, :], w_hi[:, at], start=False, stop=False)
                    last = pe.matmul(bank[h][:, :], xgT_hi[u][:, d, :], w_lo[:, at], start=False, stop=(d == DC - 1))
                last.then_inc(s[f"pre{h}_psum"], 1)

            def flip_hidden(n, h):
                pe.wait_ge(s[f"pre{h}_ready"], n + 1)
                for k in range(FC // 2):
                    c = h * FC // 2 + k
                    last = pe.transpose(bank[2 + h][:, k * P:(k + 1) * P], pre[:, c * P:(c + 1) * P], ident[:, :])
                last.then_inc(s[f"hT{h}_psum"], 1)

            def second_product(e, u, n, chunks):
                for c in chunks:
                    if c % (FC // 4) == 0:
                        pe.wait_ge(s[f"lo{c * 4 // FC}_ready"], n + 1)
                    at = bass.ds(e * WE + DC * F + c * D, D)
                    hi, lo = (w[:, c * P:(c + 1) * P] for w in (hid_hi[u], hid_lo[u]))
                    pe.matmul(bank[4 + u][:, 0:D], hi, w_hi[:, at], start=(c == 0), stop=False)
                    pe.matmul(bank[4 + u][:, 0:D], lo, w_hi[:, at], start=False, stop=False)
                    pe.matmul(bank[4 + u][:, 0:D], hi, w_lo[:, at], start=False, stop=False)

            def second_bias(e, u):
                pe.matmul(bank[4 + u][:, 0:D], ones3[:, :], b2_rows[:, bass.ds(e * D, D)], start=False, stop=True).then_inc(s["y3_psum"], 1)

            def slot(t, u, e, e_before):
                n = 2 * t + u
                pe.wait_ge(s["xgT_lo_ready"], n + 1)
                for h in range(2):
                    first_product(e, u, h)
                if e_before is not None:
                    pe.wait_ge(s["y3_ready"], n)
                for h in range(2):
                    if e_before is not None:
                        second_product(e_before, 1 - u, n - 1, range(h * FC // 2, (h + 1) * FC // 2))
                    flip_hidden(n, h)
                    if h == 0:
                        flip_rows(1 - u, t + u)
                        if u == 1:
                            load_pair(t + 1)
                if e_before is not None:
                    second_bias(e_before, 1 - u)

            even, odd, last = (pe.alloc_register(f"expert_of_{name}") for name in ("even_slot", "odd_slot", "last_slot"))

            def held(register):
                return pe.snap(register, min_val=0, max_val=E - 1)

            def load_pair(t):
                both = pe.value_load(pair_experts[0:1, bass.ds(t, 1)], min_val=0, max_val=E * E - 1)
                pe.reg_mov(even, both % E)
                pe.reg_mov(odd, both // E)

            def next_slot(t, u):
                e_before = None if isinstance(t, int) and t == u == 0 else held(last)
                e = held(odd if u else even)
                pe.reg_mov(last, e)
                slot(t, u, e, e_before)

            load_pair(0)
            next_slot(0, 0)
            next_slot(0, 1)
            with pe.Fori(1, SLOTS // 2) as t:
                for u in range(2):
                    with pe.If(2 * t + u < used):
                        next_slot(t, u)
            pe.wait_ge(s["y3_ready"], used)
            for u in range(2):
                with pe.If((used % 2 < 1) if u else (used % 2 > 0)):
                    e = held(last)
                    second_product(e, u, used - 1, range(FC))
                    second_bias(e, u)


_INS = ["x", "ctx_1024", "L0_attn_W_qk", "L0_attn_W_v", "L0_attn_alibi_slope", "L0_xattn_Wk", "L0_xattn_Wv",
        "L0_xattn_bv", "L0_xattn_Wq", "L0_xattn_bq", "L0_xattn_Wo", "L0_xattn_bo", "L0_ffn_gate_w", "L0_ffn_gate_b",
        "L0_ffn_expert_bias", "L0_ffn_w1", "L0_ffn_b1", "L0_ffn_w2", "L0_ffn_b2"]


def kernel(**inputs):
    import numpy as np
    import concourse.bacc as bacc
    from concourse.bass_utils import run_bass_kernel_spmd

    nc = bacc.Bacc("TRN2", target_bir_lowering=False, num_devices=1)
    arrays, args = {}, []
    for name in _INS:
        a = np.ascontiguousarray(inputs[name])
        arrays[f"in_{name}"] = a
        args.append(nc.dram_tensor(f"in_{name}", a.shape, mybir.dt.from_np(a.dtype), kind="ExternalInput").ap())
    out = nc.dram_tensor("out_0", inputs["x"].shape, F32, kind="ExternalOutput").ap()
    decoder_layer(nc, *args, out)
    r = run_bass_kernel_spmd(nc, [arrays], core_ids=[0])
    return r.results[0]["out_0"]
```
